# Optimizing a Trainium2 kernel written in Bass

```python
import numpy as np
import jax
import jax.numpy as jnp

def _softmax(x, axis=-1):
    return jax.nn.softmax(x, axis=axis)

def _gelu(x):
    return jax.nn.gelu(x, approximate=True)

def _silu(x):
    return jax.nn.silu(x)

def _sigmoid(x):
    return jax.nn.sigmoid(x)

def _layernorm(x, axis=-1, eps=1e-05):
    m = jnp.mean(x, axis=axis, keepdims=True)
    v = jnp.var(x, axis=axis, keepdims=True)
    return (x - m) / jnp.sqrt(v + eps)

def _scatter_add(tgt, idx, src, axis=0):
    return tgt.at[idx].add(src)

def _segment_sum(src, seg, n):
    return jax.ops.segment_sum(src, seg, n)
kernel_name = 'mk_gnn_resnorm_d1_gnn_r32_035ac2'

def setup_inputs(seed: int=0):
    np.random.seed(seed)
    _w = jnp.asarray

    def _rec_inputs():
        import jax
        import jax.numpy as jnp
        _gk = jax.random.key(seed)
        x = -0.000202 + 1 * jax.random.normal(jax.random.fold_in(_gk, 1), (50000, 128), jnp.float32)
        src = jax.random.randint(jax.random.fold_in(_gk, 2), (25000,), 0, 50000, jnp.int32)
        dst = jax.random.randint(jax.random.fold_in(_gk, 3), (25000,), 0, 50000, jnp.int32)
        _o = jnp.argsort(dst, stable=True)
        src = src[_o]
        dst = dst[_o]
        edge_weight = jax.random.uniform(jax.random.fold_in(_gk, 12), (25000,), jnp.float32, 0.0, 0.999998)
        return (x, src, dst, edge_weight)
    x, src, dst, edge_weight = _rec_inputs()

    def _L0_gnn_setup():
        import jax, jax.numpy as jnp
        import numpy as np
        N, E, H = (50000, 25000, 128)
        LN_EPS = 1e-05

        def layer_norm(x, gamma, beta):
            mu = jnp.mean(x, axis=-1, keepdims=True)
            var = jnp.mean((x - mu) ** 2, axis=-1, keepdims=True)
            return (x - mu) * jax.lax.rsqrt(var + LN_EPS) * gamma + beta
        key = jax.random.key(seed)
        ks = jax.random.split(key, 8)
        sc = 1.0 / np.sqrt(2 * H)
        return {'x': jax.random.normal(ks[0], (N, H), dtype=jnp.float32), 'edge_index': jax.random.randint(ks[1], (2, E), 0, N, dtype=jnp.int64), 'edge_weights': jax.random.uniform(ks[2], (E,), dtype=jnp.float32), 'msg_w': jax.random.normal(ks[3], (2 * H, H), dtype=jnp.float32) * sc, 'msg_b': jnp.zeros((H,), jnp.float32), 'msg_g': jnp.ones((H,), jnp.float32), 'msg_beta': jnp.zeros((H,), jnp.float32), 'upd_w': jax.random.normal(ks[4], (2 * H, H), dtype=jnp.float32) * sc, 'upd_b': jnp.zeros((H,), jnp.float32), 'upd_g': jnp.ones((H,), jnp.float32), 'upd_beta': jnp.zeros((H,), jnp.float32), 'gate_w': jax.random.normal(ks[5], (H, 1), dtype=jnp.float32) / np.sqrt(H), 'gate_b': jnp.zeros((1,), jnp.float32)}
    _L0_gnn_all = _L0_gnn_setup()
    _L0_gnn_in = {k: v for k, v in _L0_gnn_all.items() if k in ('msg_w', 'msg_b', 'msg_g', 'msg_beta', 'upd_w', 'upd_b', 'upd_g', 'upd_beta', 'gate_w', 'gate_b')}
    del _L0_gnn_all
    return {'x': x, 'src': src, 'dst': dst, 'edge_weight': edge_weight, 'L0_gnn_msg_w': _L0_gnn_in['msg_w'], 'L0_gnn_msg_b': _L0_gnn_in['msg_b'], 'L0_gnn_msg_g': _L0_gnn_in['msg_g'], 'L0_gnn_msg_beta': _L0_gnn_in['msg_beta'], 'L0_gnn_upd_w': _L0_gnn_in['upd_w'], 'L0_gnn_upd_b': _L0_gnn_in['upd_b'], 'L0_gnn_upd_g': _L0_gnn_in['upd_g'], 'L0_gnn_upd_beta': _L0_gnn_in['upd_beta'], 'L0_gnn_gate_w': _L0_gnn_in['gate_w'], 'L0_gnn_gate_b': _L0_gnn_in['gate_b']}

def reference(x, src, dst, edge_weight, L0_gnn_msg_w, L0_gnn_msg_b, L0_gnn_msg_g, L0_gnn_msg_beta, L0_gnn_upd_w, L0_gnn_upd_b, L0_gnn_upd_g, L0_gnn_upd_beta, L0_gnn_gate_w, L0_gnn_gate_b):
    import jax
    import jax.numpy as jnp

    def _L0_gnn_ref(x, edge_index, edge_weights, msg_w, msg_b, msg_g, msg_beta, upd_w, upd_b, upd_g, upd_beta, gate_w, gate_b):
        import jax, jax.numpy as jnp
        import numpy as np
        N, E, H = (50000, 25000, 128)
        LN_EPS = 1e-05

        def layer_norm(x, gamma, beta):
            mu = jnp.mean(x, axis=-1, keepdims=True)
            var = jnp.mean((x - mu) ** 2, axis=-1, keepdims=True)
            return (x - mu) * jax.lax.rsqrt(var + LN_EPS) * gamma + beta
        num_nodes = x.shape[0]
        src, dst = (edge_index[0], edge_index[1])
        em = jnp.concatenate([x[src], x[dst]], axis=-1)
        em = jax.nn.relu(layer_norm(em @ msg_w + msg_b, msg_g, msg_beta))
        em = em * edge_weights[:, None]
        msgs = jax.ops.segment_sum(em, dst, num_segments=num_nodes)
        counts = jax.ops.segment_sum(jnp.ones((src.shape[0], 1), x.dtype), dst, num_segments=num_nodes)
        valid = (counts > 0).astype(x.dtype)
        messages = msgs / (counts + 1e-08) * valid
        gate = jax.nn.sigmoid(x @ gate_w + gate_b)
        combined = jnp.concatenate([x, messages], axis=-1)
        h_new = jax.nn.relu(layer_norm(combined @ upd_w + upd_b, upd_g, upd_beta))
        return gate * h_new + (1.0 - gate) * x
    edge_index = jnp.stack([src, dst])
    x = _layernorm(x + _L0_gnn_ref(x, edge_index, edge_weight, L0_gnn_msg_w, L0_gnn_msg_b, L0_gnn_msg_g, L0_gnn_msg_beta, L0_gnn_upd_w, L0_gnn_upd_b, L0_gnn_upd_g, L0_gnn_upd_beta, L0_gnn_gate_w, L0_gnn_gate_b), axis=-1)
    return x

_drawn_inputs = setup_inputs


def setup_inputs(seed=0):
    import zlib

    import numpy as np

    out = dict(_drawn_inputs(seed))
    spreads = {'L0_gnn_msg_b': (0.0, 0.8),
     'L0_gnn_msg_g': (1.0, 0.6),
     'L0_gnn_msg_beta': (0.0, 0.8),
     'L0_gnn_upd_b': (0.0, 0.1),
     'L0_gnn_upd_g': (1.0, 0.2),
     'L0_gnn_upd_beta': (0.0, 0.298)}
    factors = {}
    for name, (base, spread) in spreads.items():
        noise = np.random.default_rng([zlib.crc32(name.encode()), seed]).standard_normal(out[name].shape)
        drawn = base * np.exp(spread * noise) if base else spread * noise
        out[name] = jnp.asarray(drawn.astype(out[name].dtype))
    for name, factor in factors.items():
        out[name] = (out[name] * factor).astype(out[name].dtype)
    return out
```

```python
from contextlib import ExitStack

import concourse.bass as bass
import numpy as np
from concourse import mybir

ALU = mybir.AluOpType
ACT = mybir.ActivationFunctionType
AX = mybir.AxisListType
F32 = mybir.dt.float32
I32 = mybir.dt.int32
BF16 = mybir.dt.bfloat16

P = 128
T = 4
LN_EPS = 1e-05
COUNT_EPS = 1e-08
REACH = 9
FAR = float(1 << 20)
LN_EXP_SET = 6
LAG = 3
ROW = P + 1


def tiles(ap):
    return ap.rearrange("p (t h) -> p t h", h=P)


def const_columns(wt):
    sizes = [P, P, 2 * T * P, 2 * T, 2, wt, 3, T, T]
    return [sum(sizes[:i]) for i in range(len(sizes) + 1)]


def gnn_kernel(nc, x, src, dst, edge_weight, msg_w, msg_b, msg_g, msg_beta,
               upd_w, upd_b, upd_g, upd_beta, gate_w, gate_b, consts, out):
    N, H = x.shape
    E, = src.shape
    ET = -(-E // P)
    EG = -(-ET // T)
    assert H == P and ET == EG * T and P < ET <= 2 * P
    BN = T * P
    NB = -(-N // BN)
    NK = NB // 2
    assert NB == 2 * NK and NK == EG and EG % 2 == 1
    WT = NB * T
    LAST = N - BN
    MSG0 = EG * BN + P
    C_IDENT, C_IOTA, C_BOUND, C_BOUNDC, C_TBASE, C_TILE, C_PART, C_LIMIT, C_NODE, C_END = const_columns(WT)

    with ExitStack() as ctx:
        def sb(name, shape, dt=F32):
            return ctx.enter_context(nc.sbuf_tensor(name, shape, dt))

        def psum(name):
            return ctx.enter_context(nc.psum_tensor(name, [P, 512], F32))

        def sem(name):
            return ctx.enter_context(nc.semaphore(name))

        rows_dram = nc.dram_tensor("rows_scratch", [MSG0 + NB * BN, ROW], F32, kind="Internal").ap()
        start_dram = nc.dram_tensor("start_scratch", [T * P], I32, kind="Internal").ap()

        const_in = sb("const_in", [P, C_END])
        ident = const_in[:, C_IDENT:C_IDENT + P]
        iota_row = const_in[:, C_IOTA:C_IOTA + P]
        tile_base = const_in[:, C_TILE:C_TILE + WT]
        ones = sb("ones", [P, P])
        ones_bf = sb("ones_bf", [P, P], BF16)
        weights = sb("weights", [P, 4, P])
        w_src, w_dst, u_x, u_msg = (weights[:, i] for i in range(4))
        w_gate = sb("w_gate", [P, 1])
        bias_rows = sb("bias_rows", [P, 2, T, P], BF16)
        columns = sb("columns", [P, 6])
        gather_idx = sb("gather_idx", [P, EG, 2 * T], I32)
        dst_col = sb("dst_col", [P, ET])
        weight_col = sb("weight_col", [P, ET])
        start_row = sb("start_row", [1, T * P], I32)

        idx_slot = [sb(f"idx_slot{s}", [P, 2 * T], I32) for s in range(2)]
        pair_rows = [sb(f"pair_rows{s}", [P, 2 * T * P]) for s in range(2)]
        xsT = sb("xsT", [P, 512])
        xdT = sb("xdT", [P, 512])
        z_stats = sb("z_stats", [P, T, 6])
        z_small = sb("z_small", [P, 4, T])
        z_ln = sb("z_ln", [P, T])
        z_rstd = sb("z_rstd", [P, T])
        zn = sb("zn", [P, 512])
        emT = sb("emT", [P, 512])
        msg_rows = [sb(f"msg_rows{s}", [P, T * ROW]) for s in range(2)]

        x_rows = [sb(f"x_rows{s}", [P, 512]) for s in range(4)]
        window = [sb(f"window{s}", [P, T * ROW]) for s in range(4)]
        xT = [sb(f"xT{s}", [P, 512]) for s in range(2)]
        onehot = [sb(f"onehot{s}", [P, 512]) for s in range(2)]
        u_stats = [sb(f"u_stats{s}", [P, T, 6]) for s in range(2)]
        u_small = [sb(f"u_small{s}", [P, 4, T]) for s in range(2)]
        u_ln = [sb(f"u_ln{s}", [P, T]) for s in range(2)]
        u_rstd = [sb(f"u_rstd{s}", [P, T]) for s in range(2)]
        gate_exp = [sb(f"gate_exp{s}", [P, T]) for s in range(2)]
        half_gate = [sb(f"half_gate{s}", [P, 2, T]) for s in range(2)]
        un = [sb(f"un{s}", [P, 512]) for s in range(2)]
        hT = [sb(f"hT{s}", [P, 512]) for s in range(2)]
        y = [sb(f"y{s}", [P, 512]) for s in range(2)]
        y_stats = [sb(f"y_stats{s}", [P, T, 6]) for s in range(2)]
        y_small = [sb(f"y_small{s}", [P, 5, T]) for s in range(2)]
        y_ln = [sb(f"y_ln{s}", [P, T]) for s in range(2)]
        y_rstd = [sb(f"y_rstd{s}", [P, T]) for s in range(2)]
        out_rows = [sb(f"out_rows{s}", [P, 512]) for s in range(2)]

        general_rows = [sb(f"general_rows{s}", [P, 2 * T * P]) for s in range(2)]
        sum_hot = [onehot[0], onehot[1], un[0], un[1]]
        block_nodes = sb("block_nodes", [P, 512])
        node_col = sb("node_col", [P, T])
        node_recip = sb("node_recip", [P, 3, T])

        ps_xs = psum("ps_xs")
        ps_xd = psum("ps_xd")
        ps_z = psum("ps_z")
        ps_t = psum("ps_t")
        ps_u = [psum("ps_u0"), psum("ps_u1")]
        ps_h = psum("ps_h")
        ps_gate = psum("ps_gate")

        w_in = sb("w_in", [P, 4, P])
        w_mean = sb("w_mean", [P, 4])
        bias_in = sb("bias_in", [P, 2, P])
        bias_mean = sb("bias_mean", [P, 2])
        bias_left = sb("bias_left", [P, 3, 2, P])
        bias_part = sb("bias_part", [P, 3, 2, P], BF16)
        bias_sum = sb("bias_sum", [P, 3, 2, P])
        halo_i = sb("halo_i", [P, 2, P + 2 * REACH], I32)
        halo = sb("halo", [P, 2, P + 2 * REACH])
        next_i = sb("next_i", [P, 2], I32)
        first_next = sb("first_next", [P, 2])
        first = sb("first", [P, 2])
        src_i = sb("src_i", [P, 2, P], I32)
        src_f = sb("src_f", [P, 2, P])
        dst_idx_f = sb("dst_idx_f", [P, 2, P])
        weight_f = sb("weight_f", [P, 2, P])
        mean_weight = sb("mean_weight", [P, 2, P])
        same = sb("same", [P, 2, P + REACH])
        count = sb("count", [P, 2, P])
        recip = sb("recip", [P, 2, P])
        odd = sb("odd", [P, 3, 2, P])
        odd_sum = sb("odd_sum", [P, 1])
        sel = sb("sel", [P, 2, 2 * T * P])
        sel_rhs = sb("sel_rhs", [P, 2, ROW])
        fine = sb("fine", [P, 2 * T])
        fine_out = sb("fine_out", [P, P])
        starts = sb("starts", [P, 2 * T])
        too_many = sb("too_many", [P, T])
        general = sb("general", [P, 1])
        general_i = sb("general_i", [P, 1], I32)
        shift = sb("shift", [P, T])
        start_f = sb("start_f", [P, T])
        start_i = sb("start_i", [P, T], I32)
        pad_rows = sb("pad_rows", [P, ROW])

        loaded, edges_loaded, consts_loaded = sem("loaded"), sem("edges_loaded"), sem("consts_loaded")
        pads_ready = sem("pads_ready")
        table_in, table_T = sem("table_in"), sem("table_T")
        setup_chain = sem("setup_chain")
        sel_ready, sel_done = sem("sel_ready"), sem("sel_done")
        odd_ready, odd_done = sem("odd_ready"), sem("odd_done")
        idx_ready, params_ready = sem("idx_ready"), sem("params_ready")
        starts_ready, start_stored, start_loaded = sem("starts_ready"), sem("start_stored"), sem("start_loaded")
        pads_stored = sem("pads_stored")
        met, weight_T, zeros_ready, sum_chain = sem("met"), sem("weight_T"), sem("zeros_ready"), sem("sum_chain")
        general_copied, general_gathered = sem("general_copied"), [sem(f"general_gathered{s}") for s in range(2)]
        group_loaded, group_hot, group_summed = sem("group_loaded"), sem("group_hot"), sem("group_summed")
        block_summed, sums_read, sums_ready, sums_stored = (
            sem("block_summed"), sem("sums_read"), sem("sums_ready"), sem("sums_stored"))

        walk_sems = []

        def walk_sem(name):
            walk_sems.append(sem(name))
            return walk_sems[-1]

        slot_copied, slot_seen = sem("slot_copied"), sem("slot_seen")
        gathered = [sem(f"gathered{s}") for s in range(2)]
        rows_stored = [walk_sem(f"rows_stored{s}") for s in range(2)]
        x_loaded = [walk_sem(f"x_loaded{s}") for s in range(4)]
        win_loaded = [walk_sem(f"win_loaded{s}") for s in range(4)]
        out_stored = [walk_sem(f"out_stored{s}") for s in range(2)]
        e1_done, e2_done, e3_done, e4_done = (walk_sem(f"e{i}_done") for i in (1, 2, 3, 4))
        n1_done, n2_done, n3_done, n4_done = (walk_sem(f"n{i}_done") for i in (1, 2, 3, 4))
        pairT_ready, z_ln_ready, z_rstd_ready, emT_ready = (
            walk_sem("pairT_ready"), walk_sem("z_ln_ready"), walk_sem("z_rstd_ready"), walk_sem("emT_ready"))
        gate_read = walk_sem("gate_read")
        xT_ready, u_ln_ready, u_rstd_ready, hT_ready, y_ln_ready, y_rstd_ready = (
            walk_sem("xT_ready"), walk_sem("u_ln_ready"), walk_sem("u_rstd_ready"), walk_sem("hT_ready"),
            walk_sem("y_ln_ready"), walk_sem("y_rstd_ready"))
        z_var_ready, zn_ready, rows_ready = walk_sem("z_var_ready"), walk_sem("zn_ready"), walk_sem("rows_ready")
        hot_ready, u_var_ready, un_ready, h_read, y_ready, y_var_ready, out_ready = (
            walk_sem("hot_ready"), walk_sem("u_var_ready"), walk_sem("un_ready"), walk_sem("h_read"), walk_sem("y_ready"),
            walk_sem("y_var_ready"), walk_sem("out_ready"))
        y_mean_ready = walk_sem("y_mean_ready")
        z_chain, u_chain, gate_chain, y_chain = walk_sem("z_chain"), walk_sem("u_chain"), walk_sem("gate_chain"), walk_sem("y_chain")

        def wait(eng, semaphore, value):
            if not (isinstance(value, int) and value <= 0):
                eng.wait_ge(semaphore, value)

        def walk(eng, step, before_pairs=None):
            for g in range(LAG):
                if before_pairs and g == LAG - 1:
                    before_pairs()
                step(g, g // 2, g % 2, None, None, None)
            for k in range(2):
                step(k + LAG, (k + LAG) // 2, (k + LAG) % 2, k, 0, k)
            with eng.Fori(1, (NK - LAG) // 2) as m:
                for ks in range(2):
                    step(2 * m + (ks + LAG), m + (ks + LAG) // 2, (ks + LAG) % 2, 2 * m + ks, m, ks)
            for k in range(NK - LAG, NK + 2):
                step(None, None, None, k, k // 2, k % 2)

        def all_edges(eng, step):
            for g in range(3):
                step(g, g // 2, g % 2, None, None, None)
            with eng.Fori(1, EG // 2) as m:
                for s in range(2):
                    step(2 * m + (s + 1), m + (s + 1) // 2, (s + 1) % 2, None, None, None)

        def meet(eng, n):
            eng.drain().then_inc(met, 1)
            eng.wait_ge(met, 5 * n)

        def is_general(eng):
            eng.wait_ge(starts_ready, 1)
            return eng.If(eng.value_load(general_i[0:1, 0:1], min_val=0, max_val=1) > 0)

        def behind(k, kh, ks, b, n):
            d = (b - n) // 2
            q = 2 * (k + d) + (b - n) % 2
            if isinstance(q, int) and not 0 <= q < NB:
                return None
            return q, (b - n) % 2, kh + (ks + d) // 2, (ks + d) % 2

        def on(task, block):
            if block is not None:
                task(*block)

        assert (NK - LAG) % 2 == 0
        block = ctx.enter_context(nc.Block())

        @block.sync
        def _(sp):
            full, rest = ET - P - 1, E - (ET - 1) * P
            by_tile = dst[0:(ET - 1) * P].rearrange("(t q) -> t q", q=P)
            before = dst[P - REACH:P - REACH + (ET - 2) * P].rearrange("(t q) -> t q", q=P)[:, 0:REACH]
            after = dst[P:(ET - 1) * P].rearrange("(t q) -> t q", q=P)[:, 0:REACH]

            def row(v, a, n):
                return v[a:a + n].rearrange("(a q) -> a q", a=1)

            def spread(v, buffer, semaphore):
                v2 = v[0:(ET - 1) * P].rearrange("(t q) -> t q", q=P)
                sp.dma_start(buffer[:, 0, :], v2[0:P]).then_inc(semaphore, 16)
                sp.dma_start(buffer[0:full, 1, :], v2[P:]).then_inc(semaphore, 16)
                sp.dma_start(buffer[full:full + 1, 1, 0:rest], row(v, (ET - 1) * P, rest)).then_inc(semaphore, 16)

            sp.dma_start(const_in[:], consts).then_inc(consts_loaded, 16)
            sp.wait_ge(pads_ready, 4)
            spread(src, src_i, edges_loaded)
            spread(dst, halo_i[:, :, REACH:REACH + P], edges_loaded)
            spread(edge_weight, weight_f, edges_loaded)
            with nc.allow_non_contiguous_dma(reason="a word for each tile"):
                for a, b in ((halo_i[1:P, 0, 0:REACH], before[0:P - 1]),
                             (halo_i[0:full, 1, 0:REACH], before[P - 1:]),
                             (halo_i[full:full + 1, 1, 0:REACH], row(dst, (ET - 1) * P - REACH, REACH)),
                             (halo_i[:, 0, REACH + P:], after[0:P]),
                             (halo_i[0:full - 1, 1, REACH + P:], after[P:]),
                             (halo_i[full - 1:full, 1, REACH + P:], row(dst, (ET - 1) * P, REACH)),
                             (next_i[:, 0:1], after[0:P, 0:1]),
                             (next_i[0:full - 1, 1:2], after[P:, 0:1]),
                             (next_i[full - 1:full, 1:2], row(dst, (ET - 1) * P, 1))):
                    sp.dma_start(a, b).then_inc(edges_loaded, 16)
            sp.wait_ge(params_ready, 1)
            sp.dma_start(rows_dram[EG * BN:MSG0, :], pad_rows[:]).then_inc(pads_stored, 16)

            sp.wait_ge(starts_ready, 1)
            with nc.allow_non_contiguous_dma(reason="512 words"):
                sp.dma_start(start_dram.rearrange("(c p) -> p c", p=P), start_i[:]).then_inc(start_stored, 16)
            sp.wait_ge(start_stored, 16)
            sp.dma_start(start_row[:], start_dram.rearrange("(a n) -> a n", a=1)).then_inc(start_loaded, 16)
            sp.wait_ge(start_loaded, 16)
            sp.wait_ge(pads_stored, 16)

            def block_rows(t, q):
                first_row = LAST if isinstance(q, int) and q == NB - 1 else q * BN
                return t[bass.ds(first_row, BN), :].rearrange("(j p) h -> p j h", p=P)

            def load_x(k, ks, b):
                sp.dma_start(tiles(x_rows[2 * ks + b][:]), block_rows(x, 2 * k + b)).then_inc(
                    x_loaded[2 * ks + b], 16)

            def load_windows(k, ks):
                for b in range(2):
                    for j in range(T):
                        at = sp.value_load(start_row[0:1, bass.ds((2 * k + b) * T + j, 1)],
                                           min_val=0, max_val=MSG0 + NB * BN - P)
                        sp.dma_start(window[2 * ks + b][:, j * ROW:(j + 1) * ROW],
                                     rows_dram[bass.ds(at, P), :]).then_inc(win_loaded[2 * ks + b], 16)

            def store_out(q, b, kh, ks):
                sp.wait_ge(out_ready, q + 1)
                if isinstance(q, int) and q == NB - 1:
                    sp.wait_ge(out_stored[0], 16 * NK)
                sp.dma_start(block_rows(out, q), tiles(out_rows[b][:])).then_inc(out_stored[b], 16)

            def load_first_pair():
                load_x(0, 0, 0)
                load_x(0, 0, 1)
                sp.wait_ge(rows_stored[0], 16)
                sp.wait_ge(rows_stored[1], 16)
                load_windows(0, 0)

            def step(g, gh, gs, k, kh, ks):
                more = k is not None and not (isinstance(k, int) and k >= NK - 1)
                if more:
                    if isinstance(k, int):
                        for s in range(2):
                            sp.wait_ge(rows_stored[s], 16 * ((min(k + 3, EG) + 1 - s) // 2))
                    else:
                        sp.wait_ge(rows_stored[ks], 16 * (kh + 2))
                        sp.wait_ge(rows_stored[1 - ks], 16 * (kh + 1 + ks))
                    wait(sp, n2_done, 2 * k)
                    load_windows(k + 1, 1 - ks)
                if k is not None:
                    on(store_out, behind(k, kh, ks, 0, 3))
                if more:
                    wait(sp, y_ready, 2 * k - 1)
                    load_x(k + 1, 1 - ks, 0)
                if g is not None:
                    sp.wait_ge(rows_ready, g + 1)
                    sp.dma_start(rows_dram[bass.ds(g * BN, BN), :].rearrange("(j p) h -> p j h", p=P),
                                 msg_rows[gs][:].rearrange("p (j h) -> p j h", h=ROW)).then_inc(rows_stored[gs], 16)
                if k is not None:
                    on(store_out, behind(k, kh, ks, 1, 3))
                if more:
                    wait(sp, y_ready, 2 * k)
                    load_x(k + 1, 1 - ks, 1)

            def sum_by_node():
                for s in range(2):
                    sp.wait_ge(rows_stored[s], 16 * ((EG + 1 - s) // 2))
                sp.sem_inc(sums_stored, 16)
                sp.sem_inc(group_summed, 1)
                sp.sem_inc(sums_read, 1)
                with sp.Fori(0, NB) as q:
                    with sp.Fori(0, EG) as g:
                        sp.wait_ge(group_summed, q * EG + g + 1)
                        sp.dma_start(window[0][:].rearrange("p (j h) -> p j h", h=ROW),
                                     rows_dram[bass.ds(g * BN, BN), :].rearrange("(j p) h -> p j h", p=P)).then_inc(
                                         group_loaded, 16)
                    sp.wait_ge(sums_ready, q + 1)
                    sp.dma_start(rows_dram[bass.ds(q * BN + MSG0, BN), :].rearrange("(j p) h -> p j h", p=P),
                                 msg_rows[0][:].rearrange("p (j h) -> p j h", h=ROW)).then_inc(sums_stored, 16)
                sp.wait_ge(sums_stored, 16 * (NB + 1))

            with is_general(sp):
                all_edges(sp, step)
                sum_by_node()
                meet(sp, 1)
                for s in walk_sems:
                    sp.sem_clear(s)
                meet(sp, 2)
            walk(sp, step, load_first_pair)
            for s in range(2):
                sp.wait_ge(out_stored[s], 16 * NK)
                sp.wait_ge(rows_stored[s], 16 * ((EG + 1 - s) // 2))

        @block.gpsimd
        def _(pool):
            def gather(g, s, before, rows, copied, gathered):
                if before is not None:
                    pool.wait_ge(e1_done, before)
                nc.gpsimd.tensor_copy(idx_slot[s][:], gather_idx[:, bass.ds(g, 1), :].rearrange(
                    "p a t -> p (a t)")).then_inc(copied, 1)
                pool.wait_ge(copied, g + 1)
                pool.sem_inc(slot_seen, 1)
                for j in range(2 * T):
                    nc.gpsimd.indirect_dma_start(
                        rows[s][:, j * P:(j + 1) * P], None, x,
                        bass.IndirectOffsetOnAxis(ap=idx_slot[s][:, j:j + 1], axis=0)).then_inc(gathered[s], 16)

            pool.wait_ge(idx_ready, 2)

            def first_gathers(*path):
                gather(0, 0, None, *path)
                gather(1, 1, None, *path)

            def other_gathers(*path):
                gather(2, 0, 1, *path)
                with nc.gpsimd.Fori(1, (EG - 1) // 2) as m:
                    for s in range(2):
                        gather(2 * m + (s + 1), (s + 1) % 2, 2 * m + s, *path)

            first_gathers(pair_rows, slot_copied, gathered)
            with is_general(pool):
                for s in range(2):
                    pool.wait_ge(gathered[s], 16 * 2 * T)
                first_gathers(general_rows, general_copied, general_gathered)
                other_gathers(general_rows, general_copied, general_gathered)
                meet(pool, 1)
                meet(pool, 2)
            other_gathers(pair_rows, slot_copied, gathered)

        @block.scalar
        def _(act):
            with nc.allow_non_contiguous_dma(reason="vectors of 128 as columns"):
                act.dma_start(weights[:, 0:2], msg_w.rearrange("(a k) h -> k a h", a=2)).then_inc(loaded, 16)
                act.dma_start(weights[:, 2:4], upd_w.rearrange("(a k) h -> k a h", a=2)).then_inc(loaded, 16)
                act.dma_start(w_gate[:], gate_w).then_inc(loaded, 16)
                for i, v in enumerate((msg_g, msg_beta, upd_g, upd_beta)):
                    act.dma_start(columns[:, i:i + 1], v.rearrange("(h a) -> h a", a=1)).then_inc(loaded, 16)
                act.dma_start(columns[:, 4:5], gate_b.rearrange("(h a) -> h a", a=1).to_broadcast([P, 1])).then_inc(
                    loaded, 16)
                for i, v in enumerate((msg_b, upd_b)):
                    act.dma_start(bias_in[:, i], v.rearrange("(a h) -> a h", a=1).to_broadcast([P, P])).then_inc(
                        loaded, 16)

            def pairT(g):
                act.wait_ge(e1_done, g + 1)
                wait(act, e2_done, g)
                nc.scalar.copy(xsT[:], ps_xs[:]).then_inc(pairT_ready, 1)
                nc.scalar.copy(xdT[:], ps_xd[:]).then_inc(pairT_ready, 1)

            def z_rstd_of(g):
                act.wait_ge(z_var_ready, g + 1)
                nc.scalar.activation(z_ln[:], z_small[:, 3], ACT.Ln, bias=LN_EPS, scale=0.25).then_inc(z_ln_ready, 1)
                act.wait_ge(z_ln_ready, g + 1)
                nc.scalar.activation(z_rstd[:], z_ln[:], ACT.Exp, scale=-0.5).then_inc(z_rstd_ready, 1)

            def emT_of(g):
                act.wait_ge(e3_done, g + 1)
                wait(act, e4_done, g)
                nc.scalar.activation(emT[:], ps_xs[:], ACT.Relu, bias=columns[:, 1:2],
                                     scale=columns[:, 0:1]).then_inc(emT_ready, 1)

            def xT_of(q, b, kh, ks):
                act.wait_ge(n1_done, q + 1)
                wait(act, n2_done, q - 1)
                nc.scalar.copy(xT[b][:], ps_t[:]).then_inc(xT_ready, 1)

            def gate_and_u_rstd(q, b, kh, ks):
                act.wait_ge(n2_done, q + 1)
                nc.scalar.activation(gate_exp[b][:], ps_gate[:, 0:T], ACT.Exp,
                                     bias=columns[:, 5:6], scale=-1.0).then_inc(gate_read, 1)
                act.wait_ge(u_var_ready, q + 1)
                nc.scalar.activation(u_ln[b][:], u_small[b][:, 3], ACT.Ln, bias=LN_EPS, scale=0.25).then_inc(
                    u_ln_ready, 1)
                act.wait_ge(u_ln_ready, q + 1)
                nc.scalar.activation(u_rstd[b][:], u_ln[b][:], ACT.Exp, scale=-0.5).then_inc(u_rstd_ready, 1)

            def hT_of(q, b, kh, ks):
                act.wait_ge(n3_done, q + 1)
                wait(act, n4_done, q - 1)
                nc.scalar.activation(hT[b][:], ps_t[:], ACT.Relu, bias=columns[:, 3:4],
                                     scale=columns[:, 2:3]).then_inc(hT_ready, 1)

            def y_rstd_of(q, b, kh, ks):
                act.wait_ge(y_var_ready, q + 1)
                nc.scalar.activation(y_ln[b][:], y_small[b][:, 3], ACT.Ln, bias=LN_EPS / 4, scale=0.25).then_inc(
                    y_ln_ready, 1)
                act.wait_ge(y_ln_ready, q + 1)
                nc.scalar.activation(y_rstd[b][:], y_ln[b][:], ACT.Exp, scale=-0.5).then_inc(y_rstd_ready, 1)

            def step(g, gh, gs, k, kh, ks):
                for b in range(2):
                    at = [behind(k, kh, ks, b, n) if k is not None else None for n in range(4)]
                    if g is not None:
                        (pairT, z_rstd_of)[b](g)
                    on(hT_of, at[2])
                    on(y_rstd_of, at[3])
                    if g is not None and b == 1:
                        emT_of(g)
                    on(xT_of, at[0])
                    on(gate_and_u_rstd, at[1])

            act.add_instruction(mybir.InstLoadActFuncSet(
                name=nc.get_next_instruction_name(), engine=mybir.EngineType.Activation,
                act_func_set_id=LN_EXP_SET))
            act.wait_ge(params_ready, 1)
            with is_general(act):
                all_edges(act, step)
                meet(act, 1)
                meet(act, 2)
            walk(act, step)

        @block.tensor
        def _(pe):
            def tile(t, j):
                return t[:, j * P:(j + 1) * P]

            pe.wait_ge(consts_loaded, 16)
            for i, (table, ps) in enumerate(((src_f, ps_t[:, 0:256]), (dst_idx_f, ps_u[1][:, 0:256]),
                                             (halo[:, :, REACH:REACH + P], ps_u[0][:, 0:256]),
                                             (mean_weight, ps_u[0][:, 256:512]))):
                pe.wait_ge(table_in, i + 1)
                for c in range(2):
                    last = nc.tensor.transpose(ps[:, c * P:(c + 1) * P], table[:, c, :], ident)
                last.then_inc(table_T, 1)
            pe.wait_ge(sel_ready, 1)
            for n in range(2 * T):
                for c in range(2):
                    last = nc.tensor.matmul([ps_xs, ps_xd, ps_z, ps_h][n // 2][:, n % 2 * ROW:(n % 2 + 1) * ROW],
                                            sel[:, c, n * P:(n + 1) * P], sel_rhs[:, c, :],
                                            start=c == 0, stop=c == 1)
            last.then_inc(sel_done, 1)
            pe.wait_ge(odd_ready, 1)
            nc.tensor.matmul(ps_gate[:, 0:1], ones[:], odd_sum[:], start=True, stop=True).then_inc(odd_done, 1)
            pe.wait_ge(params_ready, 1)
            pe.wait_ge(starts_ready, 1)

            def bias(ps, i):
                nc.tensor.matmul(ps[:], ones_bf[:], bias_rows[:, i].rearrange("p t h -> p (t h)"),
                                 start=True, stop=False, skip_group_check=True)

            def pair_transposes(g, gh, gs, rows, gathered):
                pe.wait_ge(gathered[gs], 16 * 2 * T * (gh + 1))
                wait(pe, emT_ready, g)
                wait(pe, rows_ready, g)
                for j in range(2 * T):
                    last = nc.tensor.transpose(tile((ps_xs, ps_xd)[j // T], j % T), tile(rows[gs], j), ident)
                last.then_inc(e1_done, 1)

            def message(g):
                pe.wait_ge(pairT_ready, 2 * g + 2)
                bias(ps_z, 0)
                for j in range(T):
                    nc.tensor.matmul(tile(ps_z, j), tile(xsT, j), w_src, start=False, stop=False,
                                     skip_group_check=True)
                    last = nc.tensor.matmul(tile(ps_z, j), tile(xdT, j), w_dst, start=False, stop=True,
                                            skip_group_check=True)
                last.then_inc(e2_done, 1)

            def message_transposes(g):
                pe.wait_ge(zn_ready, g + 1)
                for j in range(T):
                    last = nc.tensor.transpose(tile(ps_xs, j), tile(zn, j), ident)
                last.then_inc(e3_done, 1)

            def message_update(g):
                pe.wait_ge(emT_ready, g + 1)
                for j in range(T):
                    last = nc.tensor.matmul(tile(ps_xd, j), tile(emT, j), u_msg, start=True, stop=True)
                last.then_inc(e4_done, 1)

            def x_transposes(q, b, kh, ks):
                pe.wait_ge(x_loaded[2 * ks + b], 16 * (kh + 1))
                wait(pe, hT_ready, q - 1)
                for j in range(T):
                    last = nc.tensor.transpose(tile(ps_t, j), tile(x_rows[2 * ks + b], j), ident)
                last.then_inc(n1_done, 1)

            def update(q, b, kh, ks):
                pe.wait_ge(xT_ready, q + 1)
                pe.wait_ge(hot_ready, q + 1)
                bias(ps_u[b], 1)
                for j in range(T):
                    nc.tensor.matmul(tile(ps_u[b], j), tile(xT[b], j), u_x, start=False, stop=False,
                                     skip_group_check=True)
                    nc.tensor.matmul(tile(ps_u[b], j), tile(onehot[b], j),
                                     window[2 * ks + b][:, j * ROW:j * ROW + P], start=False, stop=True,
                                     skip_group_check=True)
                wait(pe, gate_read, q)
                for j in range(T):
                    last = nc.tensor.matmul(ps_gate[:, j:j + 1], tile(xT[b], j), w_gate[:],
                                            start=True, stop=True)
                last.then_inc(n2_done, 1)

            def update_transposes(q, b, kh, ks):
                pe.wait_ge(un_ready, q + 1)
                pe.wait_ge(xT_ready, min(q + 2, NB) if isinstance(q, int) else q + 2)
                for j in range(T):
                    last = nc.tensor.transpose(tile(ps_t, j), tile(un[b], j), ident)
                last.then_inc(n3_done, 1)

            def back_transposes(q, b, kh, ks):
                pe.wait_ge(hT_ready, q + 1)
                wait(pe, h_read, q)
                for j in range(T):
                    last = nc.tensor.transpose(tile(ps_h, j), tile(hT[b], j), ident)
                last.then_inc(n4_done, 1)

            def step(g, gh, gs, k, kh, ks, rows=pair_rows, gathered=gathered):
                for b in range(2):
                    at = [behind(k, kh, ks, b, n) if k is not None else None for n in range(4)]
                    if g is not None and b == 0:
                        pair_transposes(g, gh, gs, rows, gathered)
                    on(update_transposes, at[2])
                    on(update, at[1])
                    if g is not None and b == 1:
                        message_transposes(g)
                    on(x_transposes, at[0])
                    if g is not None:
                        (message, message_update)[b](g)
                    on(back_transposes, at[2])

            def sum_by_node():
                banks = (ps_u[0][:], xT[0][:]), (ps_gate[:, 0:T], xT[0][:, 0:T])
                with pe.Fori(0, NB) as q:
                    pe.wait_ge(sums_read, q + 1)
                    for bank, zeros in banks:
                        nc.tensor.matmul(bank, ones[:], zeros, start=True, stop=False, skip_group_check=True)
                    with pe.Fori(0, EG) as g:
                        pe.wait_ge(group_hot, q * EG + g + 1)
                        for i in range(T):
                            for j in range(T):
                                nc.tensor.matmul(tile(ps_u[0], j), tile(sum_hot[i], j),
                                                 window[0][:, i * ROW:i * ROW + P],
                                                 start=False, stop=False, skip_group_check=True)
                                last = nc.tensor.matmul(ps_gate[:, j:j + 1], tile(sum_hot[i], j), ones[:, 0:1],
                                                        start=False, stop=False, skip_group_check=True)
                        last.then_inc(group_summed, 1)
                    for bank, zeros in banks:
                        last = nc.tensor.matmul(bank, ones[:], zeros, start=False, stop=True, skip_group_check=True)
                    last.then_inc(block_summed, 1)

            with is_general(pe):
                for c in range(2):
                    last = nc.tensor.transpose(ps_u[0][:, c * P:(c + 1) * P], weight_f[:, c, :], ident)
                last.then_inc(weight_T, 1)
                all_edges(pe, lambda *at: step(*at, rows=general_rows, gathered=general_gathered))
                pe.wait_ge(zeros_ready, 1)
                sum_by_node()
                meet(pe, 1)
                meet(pe, 2)
            walk(pe, step)

        @block.vector
        def _(dve):
            links = [0]

            def link(instruction):
                links[0] += 1
                instruction.then_inc(setup_chain, 1)
                dve.wait_ge(setup_chain, links[0])

            v = nc.vector
            v.memset(halo_i[:], int(FAR)).then_inc(pads_ready, 1)
            v.memset(next_i[:], int(FAR)).then_inc(pads_ready, 1)
            v.memset(src_i[:], 0).then_inc(pads_ready, 1)
            v.memset(weight_f[:], 0.0).then_inc(pads_ready, 1)
            v.memset(ones[:], 1.0)
            v.memset(ones_bf[:], 1.0)
            v.memset(pad_rows[:, 0:P], 0.0)
            v.memset(pad_rows[:, P:ROW], FAR)
            v.memset(count[:], 1.0)
            dve.wait_ge(pads_ready, 4)
            dve.wait_ge(edges_loaded, 16 * 18)
            v.tensor_copy(src_f[:], src_i[:]).then_inc(table_in, 1)
            v.tensor_copy(first_next[:], next_i[:])
            link(v.tensor_copy(halo[:], halo_i[:]))
            here = halo[:, :, REACH:REACH + P]
            v.scalar_tensor_tensor(dst_idx_f[:], here, FAR, here, ALU.is_lt, ALU.mult).then_inc(table_in, 1)
            v.tensor_copy(first[:], halo[:, :, REACH:REACH + 1].rearrange("p c a -> p (c a)")).then_inc(table_in, 1)
            for i in range(2):
                dve.wait_ge(table_T, i + 1)
                v.tensor_copy(gather_idx[:, :, i * T:(i + 1) * T],
                              (ps_t, ps_u[1])[i][:, 0:ET].rearrange("p (g t) -> p g t", t=T)).then_inc(idx_ready, 1)
            for d in range(1, REACH + 1):
                link(v.tensor_tensor(same[:, :, 0:P + d], halo[:, :, REACH - d:REACH + P],
                                     halo[:, :, REACH:REACH + P + d], ALU.is_equal))
                link(v.tensor_tensor(count[:], count[:], same[:, :, d:d + P], ALU.add))
                link(v.tensor_tensor(count[:], count[:], same[:, :, 0:P], ALU.add))
            link(v.tensor_scalar(recip[:], count[:], COUNT_EPS, None, ALU.add))
            link(v.reciprocal(recip[:], recip[:]))
            link(v.scalar_tensor_tensor(recip[:], count[:], 0.0, recip[:], ALU.is_gt, ALU.mult))
            v.tensor_tensor(mean_weight[:], weight_f[:], recip[:], ALU.mult).then_inc(table_in, 1)
            dve.wait_ge(table_T, 4)
            v.tensor_copy(dst_col[:], ps_u[0][:, 0:ET])
            link(v.tensor_copy(weight_col[:], ps_u[0][:, 256:256 + ET]))
            dve.wait_ge(loaded, 16 * 10)
            dve.wait_ge(consts_loaded, 16)
            link(v.tensor_reduce(w_mean[:], weights[:], AX.X, ALU.add))
            link(v.tensor_scalar(w_mean[:], w_mean[:], -1.0 / P, None, ALU.mult))
            for i in range(4):
                link(v.tensor_scalar(weights[:, i], weights[:, i], w_mean[:, i:i + 1], None, ALU.add))
            link(v.tensor_reduce(bias_mean[:], bias_in[:], AX.X, ALU.add))
            link(v.tensor_scalar(bias_mean[:], bias_mean[:], -1.0 / P, None, ALU.mult))
            for i in range(2):
                link(v.tensor_scalar(bias_left[:, 0, i], bias_in[:, i], bias_mean[:, i:i + 1], None, ALU.add))
            for i in range(3):
                link(v.tensor_copy(bias_part[:, i], bias_left[:, i]))
                if i < 2:
                    link(v.tensor_tensor(bias_left[:, i + 1], bias_left[:, i], bias_part[:, i], ALU.subtract))
            mask = [const_in[:, C_PART + i:C_PART + i + 1] for i in range(3)]
            link(v.tensor_scalar(bias_sum[:, 0], bias_part[:, 0], mask[0], None, ALU.mult))
            for i in (1, 2):
                link(v.scalar_tensor_tensor(bias_sum[:, i], bias_part[:, i], mask[i], bias_sum[:, i - 1],
                                            ALU.mult, ALU.add))
            for j in range(T):
                link(v.tensor_copy(bias_rows[:, :, j, :], bias_sum[:, 2]))
            v.tensor_scalar(columns[:, 5:6], columns[:, 4:5], -1.0, None, ALU.mult).then_inc(params_ready, 1)

            v.tensor_copy(sel_rhs[:, :, 0:P], here)
            v.tensor_copy(sel_rhs[:, :, P:ROW], const_in[:, C_TBASE:C_TBASE + 2].unsqueeze(2))
            link(v.memset(first[0:1, 0:1], -1.0))
            bound = const_in[:, C_BOUND:C_BOUND + 2 * T * P]
            for c in range(2):
                link(v.tensor_scalar(sel[:, c], bound, first_next[:, c:c + 1], None, ALU.is_le))
                last = v.scalar_tensor_tensor(sel[:, c], bound, first[:, c:c + 1], sel[:, c], ALU.is_gt, ALU.mult)
            last.then_inc(sel_ready, 1)
            dve.wait_ge(sel_done, 1)
            banks = [ps_xs, ps_xd, ps_z, ps_h]
            for n in range(2 * T):
                link(v.tensor_scalar(fine_out[:], banks[n // 2][:, n % 2 * ROW:n % 2 * ROW + P],
                                     const_in[:, C_BOUNDC + n:C_BOUNDC + n + 1], None, ALU.is_lt, ALU.add,
                                     accum_out=fine[:, n:n + 1]))
            for n in range(2 * T):
                link(v.tensor_tensor(starts[:, n:n + 1], banks[n // 2][:, n % 2 * ROW + P:(n % 2 + 1) * ROW],
                                     fine[:, n:n + 1], ALU.add))
            v.tensor_tensor(odd[:, 0], here, halo[:, :, REACH + 1:REACH + 1 + P], ALU.is_gt)
            link(v.tensor_tensor(odd[:, 1], here, halo[:, :, 2 * REACH:2 * REACH + P], ALU.is_equal))
            link(v.scalar_tensor_tensor(odd[:, 1], here, FAR, odd[:, 1], ALU.is_lt, ALU.mult))
            link(v.tensor_tensor(too_many[:], starts[:, T:2 * T], starts[:, 0:T], ALU.subtract))
            v.memset(odd[:, 2], 0.0)
            link(v.tensor_scalar(too_many[:], too_many[:], float(P), None, ALU.is_gt))
            v.tensor_copy(odd[:, 2, 0, 0:T], too_many[:])
            link(v.tensor_tensor(odd[:, 2, 1, 0:T], starts[:, 0:T], const_in[:, C_LIMIT:C_LIMIT + T], ALU.is_gt))
            v.tensor_reduce(odd_sum[:], odd[:].rearrange("p a b c -> p (a b c)"), AX.X, ALU.add).then_inc(odd_ready, 1)
            dve.wait_ge(odd_done, 1)
            link(v.tensor_scalar(general[:], ps_gate[:, 0:1], 1.0, None, ALU.min))
            v.tensor_copy(general_i[:], general[:])
            link(v.tensor_tensor(shift[:], const_in[:, C_NODE:C_NODE + T], starts[:, 0:T], ALU.subtract))
            link(v.scalar_tensor_tensor(start_f[:], shift[:], general[:], starts[:, 0:T], ALU.mult, ALU.add))
            v.tensor_copy(start_i[:], start_f[:]).then_inc(starts_ready, 1)

            def variance(stats, small, chain, base):
                v.tensor_tensor(small[:, 0], stats[:, :, 2], stats[:, :, 5], ALU.add)
                v.tensor_tensor(small[:, 1], stats[:, :, 1], stats[:, :, 4], ALU.subtract).then_inc(chain, 1)
                dve.wait_ge(chain, base + 2)
                v.tensor_tensor(small[:, 2], small[:, 1], small[:, 1], ALU.mult).then_inc(chain, 1)
                dve.wait_ge(chain, base + 3)
                return v.scalar_tensor_tensor(small[:, 3], small[:, 0], 1.0 / 32, small[:, 2], ALU.mult, ALU.add)

            def row_stats(stats, rows, chain, base):
                for j in range(T):
                    last = v.bn_stats(stats[:, j], rows[:, j * P:(j + 1) * P])
                last.then_inc(chain, 1)
                dve.wait_ge(chain, base + 1)

            def by_row(column):
                return column.unsqueeze(2).to_broadcast([P, T, P])

            def z_var(g):
                dve.wait_ge(e2_done, g + 1)
                row_stats(z_stats, ps_z, z_chain, 3 * g)
                variance(z_stats, z_small, z_chain, 3 * g).then_inc(z_var_ready, 1)

            def z_norm(g):
                dve.wait_ge(z_rstd_ready, g + 1)
                wait(dve, e3_done, g)
                v.tensor_tensor(tiles(zn[:]), tiles(ps_z[:]), by_row(z_rstd[:]), ALU.mult).then_inc(zn_ready, 1)

            def rows(g, gh, gs):
                dve.wait_ge(e4_done, g + 1)
                wait(dve, rows_stored[gs], 16 * gh)
                r = msg_rows[gs][:].rearrange("p (j h) -> p j h", h=ROW)
                v.tensor_tensor(r[:, :, 0:P], tiles(ps_xd[:]), by_row(weight_col[:, bass.ds(g * T, T)]), ALU.mult)
                v.tensor_copy(r[:, :, P:ROW], dst_col[:, bass.ds(g * T, T)].unsqueeze(2)).then_inc(rows_ready, 1)

            def one_hots(q, b, kh, ks):
                dve.wait_ge(win_loaded[2 * ks + b], 16 * T * (kh + 1))
                wait(dve, n2_done, q - 1)
                for j in range(T):
                    last = v.tensor_scalar(onehot[b][:, j * P:(j + 1) * P], iota_row,
                                           tile_base[:, bass.ds(q * T + j, 1)],
                                           window[2 * ks + b][:, j * ROW + P:(j + 1) * ROW], ALU.add, ALU.is_equal)
                last.then_inc(hot_ready, 1)

            def u_var(q, b, kh, ks):
                dve.wait_ge(n2_done, q + 1)
                row_stats(u_stats[b], ps_u[b], u_chain, 3 * q)
                variance(u_stats[b], u_small[b], u_chain, 3 * q).then_inc(u_var_ready, 1)

            def u_norm(q, b, kh, ks):
                dve.wait_ge(u_rstd_ready, q + 1)
                wait(dve, n3_done, q - 1)
                v.tensor_tensor(tiles(un[b][:]), tiles(ps_u[b][:]), by_row(u_rstd[b][:]), ALU.mult).then_inc(
                    un_ready, 1)
                v.tensor_scalar(half_gate[b][:, 0], gate_exp[b][:], 2.0, 2.0, ALU.mult, ALU.add).then_inc(
                    gate_chain, 1)
                dve.wait_ge(gate_chain, 2 * q + 1)
                v.reciprocal(half_gate[b][:, 1], half_gate[b][:, 0]).then_inc(gate_chain, 1)

            def residual(q, b, kh, ks):
                dve.wait_ge(n4_done, q + 1)
                xb = x_rows[2 * ks + b]
                v.tensor_tensor(y[b][:], ps_h[:], xb[:], ALU.subtract).then_inc(h_read, 1)
                dve.wait_ge(h_read, q + 1)
                dve.wait_ge(gate_chain, 2 * q + 2)
                for j in range(T):
                    cols = slice(j * P, (j + 1) * P)
                    last = v.scalar_tensor_tensor(y[b][:, cols], y[b][:, cols], half_gate[b][:, 1, j:j + 1],
                                                  xb[:, cols], ALU.mult, ALU.add)
                last.then_inc(y_ready, 1)
                dve.wait_ge(y_ready, q + 1)
                row_stats(y_stats[b], y[b], y_chain, 3 * q)
                variance(y_stats[b], y_small[b], y_chain, 3 * q).then_inc(y_var_ready, 1)
                v.scalar_tensor_tensor(y_small[b][:, 4], y_small[b][:, 1], -0.5, y_stats[b][:, :, 1],
                                       ALU.mult, ALU.add).then_inc(y_mean_ready, 1)

            def result(q, b, kh, ks):
                dve.wait_ge(y_rstd_ready, q + 1)
                dve.wait_ge(y_mean_ready, q + 1)
                wait(dve, out_stored[b], 16 * (2 * kh + ks))
                for j in range(T):
                    cols = slice(j * P, (j + 1) * P)
                    last = v.tensor_scalar(out_rows[b][:, cols], y[b][:, cols], y_small[b][:, 4, j:j + 1],
                                           y_rstd[b][:, j:j + 1], ALU.subtract, ALU.mult)
                last.then_inc(out_ready, 1)

            def step(g, gh, gs, k, kh, ks):
                for b in range(2):
                    at = [behind(k, kh, ks, b, n) if k is not None else None for n in range(4)]
                    on(one_hots, at[0])
                    if g is not None and b == 1:
                        z_norm(g)
                    on(u_var, at[1])
                    on(result, at[3])
                    on(u_norm, at[1])
                    if g is not None:
                        if b == 0:
                            z_var(g)
                        else:
                            rows(g, gh, gs)
                    on(residual, at[2])

            def sum_by_node():
                v.memset(xT[0][:], 0.0).then_inc(zeros_ready, 1)
                for j in range(T):
                    v.tensor_scalar(block_nodes[:, j * P:(j + 1) * P], iota_row, float(j * P), None, ALU.add)
                    last = v.tensor_scalar(node_col[:, j:j + 1], const_in[:, C_TBASE:C_TBASE + 1], 1.0 / P,
                                           float(j * P), ALU.mult, ALU.add)
                last.then_inc(sum_chain, 1)
                with dve.Fori(0, NB) as q:
                    with dve.Fori(0, EG) as g:
                        dve.wait_ge(sum_chain, 5 * q + 1)
                        dve.wait_ge(group_loaded, q * (16 * EG) + g * 16 + 16)
                        for i in range(T):
                            last = v.tensor_scalar(sum_hot[i][:], block_nodes[:],
                                                   window[0][:, i * ROW + P:(i + 1) * ROW], None, ALU.is_equal)
                        last.then_inc(group_hot, 1)
                    dve.wait_ge(block_summed, q + 1)
                    dve.wait_ge(sums_stored, q * 16 + 16)
                    v.tensor_scalar(node_recip[:, 0], ps_gate[:, 0:T], COUNT_EPS, None, ALU.add).then_inc(sum_chain, 1)
                    dve.wait_ge(sum_chain, 5 * q + 2)
                    v.reciprocal(node_recip[:, 1], node_recip[:, 0]).then_inc(sum_chain, 1)
                    dve.wait_ge(sum_chain, 5 * q + 3)
                    v.scalar_tensor_tensor(node_recip[:, 2], ps_gate[:, 0:T], 0.0, node_recip[:, 1],
                                           ALU.is_gt, ALU.mult).then_inc(sum_chain, 1)
                    dve.wait_ge(sum_chain, 5 * q + 4)
                    r = msg_rows[0][:].rearrange("p (j h) -> p j h", h=ROW)
                    v.tensor_tensor(r[:, :, 0:P], tiles(ps_u[0][:]), by_row(node_recip[:, 2]), ALU.mult).then_inc(
                        sums_read, 1)
                    v.tensor_copy(r[:, :, P:ROW], node_col[:].unsqueeze(2)).then_inc(sums_ready, 1)
                    v.tensor_scalar(block_nodes[:], block_nodes[:], float(BN), None, ALU.add).then_inc(sum_chain, 1)
                    dve.wait_ge(sums_ready, q + 1)
                    v.tensor_scalar(node_col[:], node_col[:], float(BN), None, ALU.add).then_inc(sum_chain, 1)

            with is_general(dve):
                dve.wait_ge(weight_T, 1)
                link(v.tensor_copy(weight_col[:], ps_u[0][:, 0:ET]))
                all_edges(dve, step)
                sum_by_node()
                meet(dve, 1)
                meet(dve, 2)
            walk(dve, step)


def constants(n_nodes):
    blocks = -(-n_nodes // (T * P))
    wt = blocks * T
    at = const_columns(wt)
    c = np.zeros((P, at[-1]), np.float32)
    rows = np.arange(P, dtype=np.float32)
    firsts = np.concatenate([min(q * T * P, n_nodes - T * P) + P * np.arange(T) for q in range(blocks)])
    padded = np.zeros(T * P)
    padded[:wt] = firsts
    ends = np.zeros(T * P)
    ends[:wt] = firsts + P
    groups = blocks // 2
    edge_rows = groups * T * P
    limit = np.full(T * P, float(edge_rows))
    pair = np.arange(wt) // (2 * T)
    limit[:wt] = np.where(pair + 2 >= groups, edge_rows, (pair + 2) * T * P - P)
    c[:, at[0]:at[1]] = np.eye(P)
    c[:, at[1]:at[2]] = rows[None, :]
    c[:, at[2]:at[3]] = np.concatenate([padded, ends])[None, :]
    c[:, at[3]:at[4]] = np.concatenate([padded, ends]).reshape(2 * T, P).T
    c[:, at[4]] = rows * P
    c[:, at[4] + 1] = (rows + P) * P
    c[:, at[5]:at[6]] = firsts[None, :]
    c[:, at[6]:at[7]] = np.eye(P)[:, :3]
    c[:, at[7]:at[8]] = limit.reshape(T, P).T
    c[:, at[8]:at[9]] = (edge_rows + P + padded).reshape(T, P).T
    return c


_INS = ["x", "src", "dst", "edge_weight", "L0_gnn_msg_w", "L0_gnn_msg_b", "L0_gnn_msg_g", "L0_gnn_msg_beta",
        "L0_gnn_upd_w", "L0_gnn_upd_b", "L0_gnn_upd_g", "L0_gnn_upd_beta", "L0_gnn_gate_w", "L0_gnn_gate_b"]


def kernel(**inputs):
    import concourse.bacc as _bacc
    from concourse.bass_utils import run_bass_kernel_spmd as _run

    nc = _bacc.Bacc("TRN2", target_bir_lowering=False, num_devices=1)
    arrays, args = {}, []
    given = [(name, np.ascontiguousarray(inputs[name])) for name in _INS]
    given.append(("constants", constants(inputs["x"].shape[0])))
    for name, a in given:
        arrays[f"in_{name}"] = a
        args.append(nc.dram_tensor(f"in_{name}", a.shape, mybir.dt.from_np(a.dtype), kind="ExternalInput").ap())
    args.append(nc.dram_tensor("out_0", inputs["x"].shape, F32, kind="ExternalOutput").ap())
    gnn_kernel(nc, *args)
    r = _run(nc, [arrays], core_ids=[0])
    return r.results[0]["out_0"]
```

```python
from contextlib import ExitStack

import concourse.bass as bass
import numpy as np
from concourse import mybir

ALU = mybir.AluOpType
ACT = mybir.ActivationFunctionType
AX = mybir.AxisListType
F32 = mybir.dt.float32
I32 = mybir.dt.int32
BF16 = mybir.dt.bfloat16

P = 128
T = 4
LN_EPS = 1e-05
COUNT_EPS = 1e-08
REACH = 9
HALF = P // 2
SPAN = (T - 1) * HALF + P
FAR = float(1 << 20)
LN_EXP_SET = 6
LAG = 3
ROW = P + 1


def tiles(ap):
    return ap.rearrange("p (t h) -> p t h", h=P)


def const_columns(wt):
    sizes = [P, P, 2 * T * P, 2 * T, 2, wt, 3, 1, T]
    return [sum(sizes[:i]) for i in range(len(sizes) + 1)]


def gnn_kernel(nc, x, src, dst, edge_weight, msg_w, msg_b, msg_g, msg_beta,
               upd_w, upd_b, upd_g, upd_beta, gate_w, gate_b, consts, out):
    N, H = x.shape
    E, = src.shape
    ET = -(-E // P)
    EG = -(-ET // T)
    assert H == P and ET == EG * T and P < ET <= 2 * P
    BN = T * P
    NB = -(-N // BN)
    NK = NB // 2
    assert NB == 2 * NK and NK == EG and EG % 2 == 1
    WT = NB * T
    LAST = N - BN
    assert 2 * E == N
    EDGE0 = -(-(T - 1) * HALF // P) * P
    PAD0 = EDGE0 + EG * BN
    MSG0 = PAD0 + -(-SPAN // P) * P
    C_IDENT, C_IOTA, C_BOUND, C_BOUNDC, C_TBASE, C_TILE, C_PART, C_LIMIT, C_WIN, C_END = const_columns(WT)

    with ExitStack() as ctx:
        def sb(name, shape, dt=F32):
            return ctx.enter_context(nc.sbuf_tensor(name, shape, dt))

        def psum(name):
            return ctx.enter_context(nc.psum_tensor(name, [P, 512], F32))

        def sem(name):
            return ctx.enter_context(nc.semaphore(name))

        rows_dram = nc.dram_tensor("rows_scratch", [MSG0 + NB * BN, ROW], F32, kind="Internal").ap()

        const_in = sb("const_in", [P, C_END])
        ident = const_in[:, C_IDENT:C_IDENT + P]
        iota_row = const_in[:, C_IOTA:C_IOTA + P]
        tile_base = const_in[:, C_TILE:C_TILE + WT]
        ones = sb("ones", [P, P])
        ones_bf = sb("ones_bf", [P, P], BF16)
        weights = sb("weights", [P, 4, P])
        w_src, w_dst, u_msg = weights[:, 0], weights[:, 1], weights[:, 3]
        u_x_gate = sb("u_x_gate", [P, ROW])
        msg_bias, upd_bias = sb("msg_bias", [P, T, P], BF16), sb("upd_bias", [P, 2, ROW], BF16)
        columns = sb("columns", [P, 4])
        gather_idx = sb("gather_idx", [P, EG, 2 * T], I32)
        dst_col = sb("dst_col", [P, ET])
        weight_col = sb("weight_col", [P, ET])
        start_row = sb("start_row", [1, P], I32)

        idx_slot = [sb(f"idx_slot{s}", [P, 2 * T], I32) for s in range(2)]
        pair_rows = [sb(f"pair_rows{s}", [P, 2 * T * P]) for s in range(2)]
        xsT = sb("xsT", [P, 512])
        xdT = sb("xdT", [P, 512])
        squares = sb("squares", [P, 3, 512])
        z_square = sb("z_square", [P, T])
        z_ln = sb("z_ln", [P, T])
        z_rstd = sb("z_rstd", [P, T])
        zn = sb("zn", [P, 512])
        emT = sb("emT", [P, 512])
        msg_rows = [sb(f"msg_rows{s}", [P, T * ROW]) for s in range(2)]

        x_rows = [sb(f"x_rows{s}", [P, 512]) for s in range(4)]
        window = [sb(f"window{s}", [P, T * ROW]) for s in range(4)]
        xT = [sb(f"xT{s}", [P, 512]) for s in range(2)]
        onehot = [sb(f"onehot{s}", [P, 512]) for s in range(2)]
        u_square = [sb(f"u_square{s}", [P, T]) for s in range(2)]
        u_ln = [sb(f"u_ln{s}", [P, T]) for s in range(2)]
        u_rstd = [sb(f"u_rstd{s}", [P, T]) for s in range(2)]
        gate_exp = [sb(f"gate_exp{s}", [P, T]) for s in range(2)]
        gate_small = [sb(f"gate_small{s}", [P, 3, T]) for s in range(2)]
        dst_place = [sb(f"dst_place{s}", [P, T]) for s in range(2)]
        un = [sb(f"un{s}", [P, 512]) for s in range(2)]
        hT = [sb(f"hT{s}", [P, 512]) for s in range(2)]
        y = [sb(f"y{s}", [P, 512]) for s in range(2)]
        y_stats = [sb(f"y_stats{s}", [P, T, 6]) for s in range(2)]
        y_small = [sb(f"y_small{s}", [P, 6, T]) for s in range(2)]
        y_ln = [sb(f"y_ln{s}", [P, T]) for s in range(2)]
        y_rstd = [sb(f"y_rstd{s}", [P, T]) for s in range(2)]
        out_rows = [sb(f"out_rows{s}", [P, 512]) for s in range(2)]

        general_rows = [sb(f"general_rows{s}", [P, 2 * T * P]) for s in range(2)]
        sum_hot = [onehot[0], onehot[1], un[0], un[1]]
        block_nodes = sb("block_nodes", [P, 512])
        node_col = sb("node_col", [P, T])
        node_recip = sb("node_recip", [P, 3, T])

        ps_xs = psum("ps_xs")
        ps_xd = psum("ps_xd")
        ps_z = psum("ps_z")
        ps_x = psum("ps_x")
        ps_t = psum("ps_t")
        ps_u = ctx.enter_context(nc.psum_tensor("ps_u", [P, 1024], F32))
        ps_h = psum("ps_h")

        def u_tile(j, n):
            return ps_u[:, (j // 2) * 512 + (j % 2) * ROW:][:, 0:n]

        u_by_bank = ps_u[:].rearrange("p (a c) -> p a c", a=2)[:, :, 0:2 * ROW].rearrange(
            "p a (t h) -> p a t h", h=ROW)
        u_gates = u_by_bank[:, :, :, P:ROW]

        w_in = sb("w_in", [P, 4, P])
        w_mean = sb("w_mean", [P, 4])
        bias_in = sb("bias_in", [P, 2, ROW])
        bias_mean = sb("bias_mean", [P, 2])
        bias_left = sb("bias_left", [P, 3, 2, ROW])
        bias_part = sb("bias_part", [P, 3, 2, ROW], BF16)
        bias_sum = sb("bias_sum", [P, 3, 2, ROW])
        halo_i = sb("halo_i", [P, 2, P + 2 * REACH], I32)
        halo = sb("halo", [P, 2, P + 2 * REACH])
        next_i = sb("next_i", [P, 2], I32)
        first_next = sb("first_next", [P, 2])
        first = sb("first", [P, 2])
        src_i = sb("src_i", [P, 2, P], I32)
        src_f = sb("src_f", [P, 2, P])
        dst_idx_f = sb("dst_idx_f", [P, 2, P])
        weight_f = sb("weight_f", [P, 2, P])
        mean_weight = sb("mean_weight", [P, 2, P])
        same = sb("same", [P, 2, P + REACH])
        count = sb("count", [P, 2, P])
        recip = sb("recip", [P, 2, P])
        odd = sb("odd", [P, 3, 2, P])
        odd_sum = sb("odd_sum", [P, 1])
        sel = sb("sel", [P, 2, 2 * T * P])
        sel_rhs = sb("sel_rhs", [P, 2, ROW])
        fine = sb("fine", [P, 2 * T])
        fine_out = sb("fine_out", [P, P])
        starts = sb("starts", [P, 2 * T])
        ends = sb("ends", [P, T])
        block_start = sb("block_start", [P, 1])
        general = sb("general", [P, 1])
        general_i = sb("general_i", [P, 1], I32)
        pad_rows = sb("pad_rows", [P, ROW])

        loaded, edges_loaded, consts_loaded = sem("loaded"), sem("edges_loaded"), sem("consts_loaded")
        pads_ready = sem("pads_ready")
        table_in, table_T = sem("table_in"), sem("table_T")
        setup_chain = sem("setup_chain")
        sel_ready, sel_done = sem("sel_ready"), sem("sel_done")
        odd_ready, odd_done = sem("odd_ready"), sem("odd_done")
        idx_ready, params_ready = sem("idx_ready"), sem("params_ready")
        block_starts_ready, starts_T, starts_ready = sem("block_starts_ready"), sem("starts_T"), sem("starts_ready")
        pads_stored = sem("pads_stored")
        met, weight_T, zeros_ready, sum_chain = sem("met"), sem("weight_T"), sem("zeros_ready"), sem("sum_chain")
        general_copied, general_gathered = sem("general_copied"), [sem(f"general_gathered{s}") for s in range(2)]
        group_loaded, group_hot, group_summed = sem("group_loaded"), sem("group_hot"), sem("group_summed")
        block_summed, sums_read, sums_ready, sums_stored = (
            sem("block_summed"), sem("sums_read"), sem("sums_ready"), sem("sums_stored"))

        walk_sems = []

        def walk_sem(name):
            walk_sems.append(sem(name))
            return walk_sems[-1]

        slot_copied, slot_seen = sem("slot_copied"), sem("slot_seen")
        gathered = [sem(f"gathered{s}") for s in range(2)]
        rows_stored = [walk_sem(f"rows_stored{s}") for s in range(2)]
        x_loaded = [walk_sem(f"x_loaded{s}") for s in range(4)]
        win_loaded = [walk_sem(f"win_loaded{s}") for s in range(4)]
        out_stored = [walk_sem(f"out_stored{s}") for s in range(2)]
        e1_done, e2_done, e3_done, e4_done = (walk_sem(f"e{i}_done") for i in (1, 2, 3, 4))
        n1_done, n2_done, n3_done, n4_done = (walk_sem(f"n{i}_done") for i in (1, 2, 3, 4))
        pairT_ready, z_ln_ready, z_rstd_ready, emT_ready = (
            walk_sem("pairT_ready"), walk_sem("z_ln_ready"), walk_sem("z_rstd_ready"), walk_sem("emT_ready"))
        gate_exp_ready = walk_sem("gate_exp_ready")
        xT_ready, u_ln_ready, u_rstd_ready, hT_ready, y_ln_ready, y_rstd_ready = (
            walk_sem("xT_ready"), walk_sem("u_ln_ready"), walk_sem("u_rstd_ready"), walk_sem("hT_ready"),
            walk_sem("y_ln_ready"), walk_sem("y_rstd_ready"))
        zn_ready, rows_ready = walk_sem("zn_ready"), walk_sem("rows_ready")
        hot_ready, un_ready, y_ready, y_var_ready, out_ready = (
            walk_sem("hot_ready"), walk_sem("un_ready"), walk_sem("y_ready"),
            walk_sem("y_var_ready"), walk_sem("out_ready"))
        y_mean_ready = walk_sem("y_mean_ready")
        place_chain, gate_chain, y_chain = walk_sem("place_chain"), walk_sem("gate_chain"), walk_sem("y_chain")
        z_square_ready, u_square_ready = walk_sem("z_square_ready"), walk_sem("u_square_ready")

        def wait(eng, semaphore, value):
            if not (isinstance(value, int) and value <= 0):
                eng.wait_ge(semaphore, value)

        def walk(eng, step, before_pairs=None):
            for g in range(LAG):
                step(g, g // 2, g % 2, None, None, None)
            if before_pairs:
                before_pairs()
            for k in range(2):
                step(k + LAG, (k + LAG) // 2, (k + LAG) % 2, k, 0, k)
            with eng.Fori(1, (NK - LAG) // 2) as m:
                for ks in range(2):
                    step(2 * m + (ks + LAG), m + (ks + LAG) // 2, (ks + LAG) % 2, 2 * m + ks, m, ks)
            for k in range(NK - LAG, NK + 2):
                g = k + LAG
                step(*((g, g // 2, g % 2) if g == EG else (None, None, None)), k, k // 2, k % 2)

        def all_edges(eng, step):
            for g in range(3):
                step(g, g // 2, g % 2, None, None, None)
            with eng.Fori(1, EG // 2) as m:
                for s in range(2):
                    step(2 * m + (s + 1), m + (s + 1) // 2, (s + 1) % 2, None, None, None)
            step(EG, EG // 2, EG % 2, None, None, None)

        def meet(eng, n):
            eng.drain().then_inc(met, 1)
            eng.wait_ge(met, 5 * n)

        def is_general(eng):
            eng.wait_ge(starts_ready, 1)
            return eng.If(eng.value_load(general_i[0:1, 0:1], min_val=0, max_val=1) > 0)

        def behind(k, kh, ks, b, n):
            d = (b - n) // 2
            q = 2 * (k + d) + (b - n) % 2
            if isinstance(q, int) and not 0 <= q < NB:
                return None
            return q, (b - n) % 2, kh + (ks + d) // 2, (ks + d) % 2

        def group(g, gh, gs, n):
            if g is None or (isinstance(g, int) and not 0 <= g - n < EG):
                return None
            return g - n, gh + (gs - n) // 2, (gs - n) % 2

        def on(task, block):
            if block is not None:
                task(*block)

        assert (NK - LAG) % 2 == 0
        block = ctx.enter_context(nc.Block())

        @block.sync
        def _(sp):
            full, rest = ET - P - 1, E - (ET - 1) * P
            by_tile = dst[0:(ET - 1) * P].rearrange("(t q) -> t q", q=P)
            before = dst[P - REACH:P - REACH + (ET - 2) * P].rearrange("(t q) -> t q", q=P)[:, 0:REACH]
            after = dst[P:(ET - 1) * P].rearrange("(t q) -> t q", q=P)[:, 0:REACH]

            def row(v, a, n):
                return v[a:a + n].rearrange("(a q) -> a q", a=1)

            def spread(v, buffer, semaphore):
                v2 = v[0:(ET - 1) * P].rearrange("(t q) -> t q", q=P)
                sp.dma_start(buffer[:, 0, :], v2[0:P]).then_inc(semaphore, 16)
                sp.dma_start(buffer[0:full, 1, :], v2[P:]).then_inc(semaphore, 16)
                sp.dma_start(buffer[full:full + 1, 1, 0:rest], row(v, (ET - 1) * P, rest)).then_inc(semaphore, 16)

            sp.dma_start(const_in[:], consts).then_inc(consts_loaded, 16)
            sp.wait_ge(pads_ready, 4)
            spread(src, src_i, edges_loaded)
            spread(dst, halo_i[:, :, REACH:REACH + P], edges_loaded)
            spread(edge_weight, weight_f, edges_loaded)
            with nc.allow_non_contiguous_dma(reason="a word for each tile"):
                for a, b in ((halo_i[1:P, 0, 0:REACH], before[0:P - 1]),
                             (halo_i[0:full, 1, 0:REACH], before[P - 1:]),
                             (halo_i[full:full + 1, 1, 0:REACH], row(dst, (ET - 1) * P - REACH, REACH)),
                             (halo_i[:, 0, REACH + P:], after[0:P]),
                             (halo_i[0:full - 1, 1, REACH + P:], after[P:]),
                             (halo_i[full - 1:full, 1, REACH + P:], row(dst, (ET - 1) * P, REACH)),
                             (next_i[:, 0:1], after[0:P, 0:1]),
                             (next_i[0:full - 1, 1:2], after[P:, 0:1]),
                             (next_i[full - 1:full, 1:2], row(dst, (ET - 1) * P, 1))):
                    sp.dma_start(a, b).then_inc(edges_loaded, 16)
            sp.wait_ge(params_ready, 1)
            pads = [*range(0, EDGE0, P), *range(PAD0, MSG0, P)]
            for a in pads:
                sp.dma_start(rows_dram[a:a + P, :], pad_rows[:]).then_inc(pads_stored, 16)
            sp.wait_ge(pads_stored, 16 * len(pads))

            def block_rows(t, q, half=None):
                first_row = LAST if isinstance(q, int) and q == NB - 1 else q * BN
                if half is None:
                    return t[bass.ds(first_row, BN), :].rearrange("(j p) h -> p j h", p=P)
                return t[bass.ds(first_row + half * (BN // 2), BN // 2), :].rearrange("(j p) h -> p j h", p=P)

            def load_x(k, ks, b):
                sp.dma_start(tiles(x_rows[2 * ks + b][:]), block_rows(x, 2 * k + b)).then_inc(
                    x_loaded[2 * ks + b], 16)

            def load_windows(k, ks):
                for b in range(2):
                    at = sp.value_load(start_row[0:1, bass.ds(2 * k + b, 1)], min_val=0, max_val=MSG0 - SPAN)
                    for i in range(2):
                        sp.dma_start(window[2 * ks + b][:].rearrange("p (a i h) -> p i a h", i=2, h=ROW)[:, i],
                                     rows_dram[bass.ds(at + i * HALF, 2 * P), :].rearrange(
                                         "(a p) h -> p a h", p=P)).then_inc(win_loaded[2 * ks + b], 16)

            def load_node_rows(k, ks):
                for b in range(2):
                    for i in range(2):
                        sp.dma_start(window[2 * ks + b][:].rearrange("p (i a h) -> p i a h", i=2, h=ROW)[:, i],
                                     block_rows(rows_dram[MSG0:], 2 * k + b, i)).then_inc(win_loaded[2 * ks + b], 16)

            def store_out(q, b, kh, ks):
                sp.wait_ge(out_ready, q + 1)
                if isinstance(q, int) and q == NB - 1:
                    sp.wait_ge(out_stored[0], 16 * NK)
                sp.dma_start(block_rows(out, q), tiles(out_rows[b][:])).then_inc(out_stored[b], 16)

            def store_rows(g, gh, gs):
                sp.wait_ge(rows_ready, g + 1)
                sp.dma_start(rows_dram[bass.ds(g * BN + EDGE0, BN), :].rearrange("(j p) h -> p j h", p=P),
                             msg_rows[gs][:].rearrange("p (j h) -> p j h", h=ROW)).then_inc(rows_stored[gs], 16)

            def load_first_pair(load_messages=load_windows):
                load_x(0, 0, 0)
                load_x(0, 0, 1)
                sp.wait_ge(rows_stored[0], 16)
                sp.wait_ge(rows_stored[1], 16)
                load_messages(0, 0)

            def step(g, gh, gs, k, kh, ks, load_messages=load_windows):
                more = k is not None and not (isinstance(k, int) and k >= NK - 1)
                if k is not None:
                    on(store_out, behind(k, kh, ks, 0, 3))
                if more:
                    wait(sp, y_ready, 2 * k - 1)
                    load_x(k + 1, 1 - ks, 0)
                on(store_rows, group(g, gh, gs, 1))
                if k is not None:
                    on(store_out, behind(k, kh, ks, 1, 3))
                if more:
                    if isinstance(k, int):
                        for s in range(2):
                            sp.wait_ge(rows_stored[s], 16 * ((min(k + 3, EG) + 1 - s) // 2))
                    else:
                        sp.wait_ge(rows_stored[ks], 16 * (kh + 2))
                        sp.wait_ge(rows_stored[1 - ks], 16 * (kh + 1 + ks))
                    wait(sp, gate_exp_ready, 2 * k)
                    load_messages(k + 1, 1 - ks)
                    wait(sp, y_ready, 2 * k)
                    load_x(k + 1, 1 - ks, 1)

            def sum_by_node():
                for s in range(2):
                    sp.wait_ge(rows_stored[s], 16 * ((EG + 1 - s) // 2))
                sp.sem_inc(sums_stored, 16)
                sp.sem_inc(group_summed, 1)
                sp.sem_inc(sums_read, 1)
                with sp.Fori(0, NB) as q:
                    with sp.Fori(0, EG) as g:
                        sp.wait_ge(group_summed, q * EG + g + 1)
                        sp.dma_start(window[0][:].rearrange("p (j h) -> p j h", h=ROW),
                                     rows_dram[bass.ds(g * BN + EDGE0, BN), :].rearrange("(j p) h -> p j h", p=P)).then_inc(
                                         group_loaded, 16)
                    sp.wait_ge(sums_ready, q + 1)
                    sp.dma_start(rows_dram[bass.ds(q * BN + MSG0, BN), :].rearrange("(j p) h -> p j h", p=P),
                                 msg_rows[0][:].rearrange("p (j h) -> p j h", h=ROW)).then_inc(sums_stored, 16)
                sp.wait_ge(sums_stored, 16 * (NB + 1))

            sp.wait_ge(starts_ready, 1)
            with is_general(sp):
                all_edges(sp, step)
                sum_by_node()
                meet(sp, 1)
                for s in walk_sems:
                    sp.sem_clear(s)
                meet(sp, 2)
                walk(sp, lambda *at: step(*at, load_messages=load_node_rows),
                     lambda: load_first_pair(load_node_rows))
            with sp.Else():
                walk(sp, step, load_first_pair)
            for s in range(2):
                sp.wait_ge(out_stored[s], 16 * NK)
                sp.wait_ge(rows_stored[s], 16 * ((EG + 1 - s) // 2))

        @block.gpsimd
        def _(pool):
            def gather(g, s, before, rows, copied, gathered):
                if before is not None:
                    pool.wait_ge(e1_done, before)
                nc.gpsimd.tensor_copy(idx_slot[s][:], gather_idx[:, bass.ds(g, 1), :].rearrange(
                    "p a t -> p (a t)")).then_inc(copied, 1)
                pool.wait_ge(copied, g + 1)
                pool.sem_inc(slot_seen, 1)
                for j in range(2 * T):
                    nc.gpsimd.indirect_dma_start(
                        rows[s][:, j * P:(j + 1) * P], None, x,
                        bass.IndirectOffsetOnAxis(ap=idx_slot[s][:, j:j + 1], axis=0)).then_inc(gathered[s], 16)

            pool.wait_ge(idx_ready, 2)

            def first_gathers(*path):
                gather(0, 0, None, *path)
                gather(1, 1, None, *path)

            def other_gathers(*path):
                gather(2, 0, 1, *path)
                with nc.gpsimd.Fori(1, (EG - 1) // 2) as m:
                    for s in range(2):
                        gather(2 * m + (s + 1), (s + 1) % 2, 2 * m + s, *path)

            first_gathers(pair_rows, slot_copied, gathered)
            with is_general(pool):
                for s in range(2):
                    pool.wait_ge(gathered[s], 16 * 2 * T)
                first_gathers(general_rows, general_copied, general_gathered)
                other_gathers(general_rows, general_copied, general_gathered)
                meet(pool, 1)
                meet(pool, 2)
            other_gathers(pair_rows, slot_copied, gathered)

        @block.scalar
        def _(act):
            with nc.allow_non_contiguous_dma(reason="vectors of 128 as columns"):
                act.dma_start(weights[:, 0:2], msg_w.rearrange("(a k) h -> k a h", a=2)).then_inc(loaded, 16)
                act.dma_start(weights[:, 2:4], upd_w.rearrange("(a k) h -> k a h", a=2)).then_inc(loaded, 16)
                act.dma_start(u_x_gate[:, P:ROW], gate_w).then_inc(loaded, 16)
                for i, v in enumerate((msg_g, msg_beta, upd_g, upd_beta)):
                    act.dma_start(columns[:, i:i + 1], v.rearrange("(h a) -> h a", a=1)).then_inc(loaded, 16)
                act.dma_start(bias_in[:, 1, P:ROW], gate_b.rearrange("(h a) -> h a", a=1).to_broadcast([P, 1])).then_inc(
                    loaded, 16)
                for i, v in enumerate((msg_b, upd_b)):
                    act.dma_start(bias_in[:, i, 0:P], v.rearrange("(a h) -> a h", a=1).to_broadcast([P, P])).then_inc(
                        loaded, 16)

            def pairT(g, gh, gs):
                act.wait_ge(e1_done, g + 1)
                wait(act, e2_done, g)
                nc.scalar.copy(xsT[:], ps_xs[:]).then_inc(pairT_ready, 1)
                nc.scalar.copy(xdT[:], ps_xd[:]).then_inc(pairT_ready, 1)

            def z_rstd_of(g, gh, gs):
                act.wait_ge(e2_done, g + 1)
                for j in range(T):
                    last = nc.scalar.activation(squares[:, 2, j * P:(j + 1) * P], ps_z[:, j * P:(j + 1) * P], ACT.Square,
                                                accum_out=z_square[:, j:j + 1])
                last.then_inc(z_square_ready, 1)
                act.wait_ge(z_square_ready, g + 1)
                nc.scalar.activation(z_ln[:], z_square[:], ACT.Ln, bias=LN_EPS, scale=1.0 / P).then_inc(z_ln_ready, 1)
                act.wait_ge(z_ln_ready, g + 1)
                nc.scalar.activation(z_rstd[:], z_ln[:], ACT.Exp, scale=-0.5).then_inc(z_rstd_ready, 1)

            def emT_of(g, gh, gs):
                act.wait_ge(e3_done, g + 1)
                wait(act, e4_done, g)
                nc.scalar.activation(emT[:], ps_xs[:], ACT.Relu, bias=columns[:, 1:2],
                                     scale=columns[:, 0:1]).then_inc(emT_ready, 1)

            def xT_of(q, b, kh, ks):
                act.wait_ge(n1_done, q + 1)
                wait(act, n2_done, 2 * q - 2)
                nc.scalar.copy(xT[b][:], ps_x[:]).then_inc(xT_ready, 1)

            def gates_and_squares(q, b, kh, ks):
                for a in range(2):
                    act.wait_ge(n2_done, 2 * q + a + 1)
                    for j in (2 * a, 2 * a + 1):
                        last = nc.scalar.activation(squares[:, b, j * P:(j + 1) * P], u_tile(j, P), ACT.Square,
                                                    accum_out=u_square[b][:, j:j + 1])
                last.then_inc(u_square_ready, 1)
                nc.scalar.activation(gate_exp[b][:].rearrange("p (a t) -> p a t", a=2).unsqueeze(3), u_gates,
                                     ACT.Exp, scale=-1.0).then_inc(gate_exp_ready, 1)

            def rstds(y_block, u_block):
                if y_block is not None:
                    q, b = y_block[:2]
                    act.wait_ge(y_var_ready, q + 1)
                    nc.scalar.activation(y_ln[b][:], y_small[b][:, 4], ACT.Ln, bias=LN_EPS / 4,
                                         scale=1.0 / P).then_inc(y_ln_ready, 1)
                if u_block is not None:
                    q, b = u_block[:2]
                    act.wait_ge(u_square_ready, q + 1)
                    nc.scalar.activation(u_ln[b][:], u_square[b][:], ACT.Ln, bias=LN_EPS,
                                         scale=1.0 / P).then_inc(u_ln_ready, 1)
                if y_block is not None:
                    q, b = y_block[:2]
                    act.wait_ge(y_ln_ready, q + 1)
                    nc.scalar.activation(y_rstd[b][:], y_ln[b][:], ACT.Exp, scale=-0.5).then_inc(y_rstd_ready, 1)
                if u_block is not None:
                    q, b = u_block[:2]
                    act.wait_ge(u_ln_ready, q + 1)
                    nc.scalar.activation(u_rstd[b][:], u_ln[b][:], ACT.Exp, scale=-0.5).then_inc(u_rstd_ready, 1)

            def u_norm(q, b, kh, ks):
                act.wait_ge(u_rstd_ready, q + 1)
                wait(act, n3_done, q - 1)
                for a in range(2):
                    for j in (2 * a, 2 * a + 1):
                        last = nc.scalar.activation(un[b][:, j * P:(j + 1) * P], u_tile(j, P), ACT.Copy,
                                                    scale=u_rstd[b][:, j:j + 1])
                    last.then_inc(un_ready, 1)

            def hT_of(q, b, kh, ks):
                act.wait_ge(n3_done, q + 1)
                wait(act, n4_done, q - 1)
                nc.scalar.activation(hT[b][:], ps_t[:], ACT.Relu, bias=columns[:, 3:4],
                                     scale=columns[:, 2:3]).then_inc(hT_ready, 1)

            def step(g, gh, gs, k, kh, ks):
                this, former = group(g, gh, gs, 0), group(g, gh, gs, 1)
                for b in range(2):
                    at = [behind(k, kh, ks, b, n) if k is not None else None for n in range(4)]
                    on(xT_of, at[0])
                    on(gates_and_squares, at[1])
                    rstds(at[3], at[1])
                    on(hT_of, at[2])
                    if b == 0:
                        on(emT_of, former)
                    on(u_norm, at[1])
                    on((pairT, z_rstd_of)[b], this)

            act.add_instruction(mybir.InstLoadActFuncSet(
                name=nc.get_next_instruction_name(), engine=mybir.EngineType.Activation,
                act_func_set_id=LN_EXP_SET))
            with is_general(act):
                all_edges(act, step)
                meet(act, 1)
                meet(act, 2)
            walk(act, step)

        @block.tensor
        def _(pe):
            def tile(t, j):
                return t[:, j * P:(j + 1) * P]

            pe.wait_ge(consts_loaded, 16)
            for i, (table, ps) in enumerate(((src_f, ps_t[:, 0:256]), (dst_idx_f, ps_u[:, 512:768]),
                                             (halo[:, :, REACH:REACH + P], ps_u[:, 0:256]),
                                             (mean_weight, ps_u[:, 256:512]))):
                pe.wait_ge(table_in, i + 1)
                for c in range(2):
                    last = nc.tensor.transpose(ps[:, c * P:(c + 1) * P], table[:, c, :], ident)
                last.then_inc(table_T, 1)
            pe.wait_ge(sel_ready, 1)
            for n in range(2 * T):
                for c in range(2):
                    last = nc.tensor.matmul([ps_xs, ps_xd, ps_z, ps_h][n // 2][:, n % 2 * ROW:(n % 2 + 1) * ROW],
                                            sel[:, c, n * P:(n + 1) * P], sel_rhs[:, c, :],
                                            start=c == 0, stop=c == 1)
            last.then_inc(sel_done, 1)
            pe.wait_ge(block_starts_ready, 1)
            nc.tensor.transpose(ps_t[0:1, 0:P], block_start[:], ident).then_inc(starts_T, 1)
            pe.wait_ge(odd_ready, 1)
            nc.tensor.matmul(ps_x[:, 0:1], ones[:], odd_sum[:], start=True, stop=True).then_inc(odd_done, 1)
            pe.wait_ge(params_ready, 1)
            pe.wait_ge(starts_ready, 1)

            def bias(bank, rows):
                nc.tensor.matmul(bank, ones_bf[:], rows[:].rearrange("p t h -> p (t h)"),
                                 start=True, stop=False, skip_group_check=True)

            def pair_transposes(g, gh, gs, rows, gathered):
                pe.wait_ge(gathered[gs], 16 * 2 * T * (gh + 1))
                wait(pe, pairT_ready, 2 * g)
                wait(pe, emT_ready, g)
                for j in range(2 * T):
                    last = nc.tensor.transpose(tile((ps_xs, ps_xd)[j // T], j % T), tile(rows[gs], j), ident)
                last.then_inc(e1_done, 1)

            def message(g, gh, gs):
                pe.wait_ge(pairT_ready, 2 * g + 2)
                wait(pe, rows_ready, g)
                bias(ps_z[:], msg_bias)
                for j in range(T):
                    nc.tensor.matmul(tile(ps_z, j), tile(xsT, j), w_src, start=False, stop=False,
                                     skip_group_check=True)
                    last = nc.tensor.matmul(tile(ps_z, j), tile(xdT, j), w_dst, start=False, stop=True,
                                            skip_group_check=True)
                last.then_inc(e2_done, 1)

            def message_transposes(g, gh, gs):
                pe.wait_ge(zn_ready, g + 1)
                for j in range(T):
                    last = nc.tensor.transpose(tile(ps_xs, j), tile(zn, j), ident)
                last.then_inc(e3_done, 1)

            def message_update(g, gh, gs):
                pe.wait_ge(emT_ready, g + 1)
                for j in range(T):
                    last = nc.tensor.matmul(tile(ps_z, j), tile(emT, j), u_msg, start=True, stop=True)
                last.then_inc(e4_done, 1)

            def x_transposes(q, b, kh, ks):
                pe.wait_ge(x_loaded[2 * ks + b], 16 * (kh + 1))
                wait(pe, xT_ready, q)
                for j in range(T):
                    last = nc.tensor.transpose(tile(ps_x, j), tile(x_rows[2 * ks + b], j), ident)
                last.then_inc(n1_done, 1)

            def update(q, b, kh, ks):
                pe.wait_ge(xT_ready, q + 1)
                pe.wait_ge(hot_ready, q + 1)
                for a in range(2):
                    wait(pe, un_ready, 2 * q - 1 + a)
                    bias(ps_u[:, a * 512:a * 512 + 2 * ROW], upd_bias)
                    for j in (2 * a, 2 * a + 1):
                        nc.tensor.matmul(u_tile(j, ROW), tile(xT[b], j), u_x_gate[:], start=False, stop=False,
                                         skip_group_check=True)
                        last = nc.tensor.matmul(u_tile(j, P), tile(onehot[b], j),
                                                window[2 * ks + b][:, j * ROW:j * ROW + P], start=False, stop=True,
                                                skip_group_check=True)
                    last.then_inc(n2_done, 1)

            def update_transposes(q, b, kh, ks):
                pe.wait_ge(un_ready, 2 * q + 2)
                wait(pe, hT_ready, q)
                for j in range(T):
                    last = nc.tensor.transpose(tile(ps_t, j), tile(un[b], j), ident)
                last.then_inc(n3_done, 1)

            def back_transposes(q, b, kh, ks):
                pe.wait_ge(hT_ready, q + 1)
                wait(pe, y_ready, q)
                for j in range(T):
                    last = nc.tensor.transpose(tile(ps_h, j), tile(hT[b], j), ident)
                last.then_inc(n4_done, 1)

            def step(g, gh, gs, k, kh, ks, rows=pair_rows, gathered=gathered):
                this, former = group(g, gh, gs, 0), group(g, gh, gs, 1)
                for b in range(2):
                    at = [behind(k, kh, ks, b, n) if k is not None else None for n in range(4)]
                    on(x_transposes, at[0])
                    on(update, at[1])
                    on(update_transposes, at[2])
                    on(*((message_transposes, former) if b == 0 else (message, this)))
                    on(back_transposes, at[2])
                    if b == 0:
                        on(message_update, former)
                        if this is not None:
                            pair_transposes(*this, rows, gathered)

            def sum_by_node():
                banks = (ps_t[:], xT[0][:]), (ps_x[:, 0:T], xT[0][:, 0:T])
                with pe.Fori(0, NB) as q:
                    pe.wait_ge(sums_read, q + 1)
                    for bank, zeros in banks:
                        nc.tensor.matmul(bank, ones[:], zeros, start=True, stop=False, skip_group_check=True)
                    with pe.Fori(0, EG) as g:
                        pe.wait_ge(group_hot, q * EG + g + 1)
                        for i in range(T):
                            for j in range(T):
                                nc.tensor.matmul(tile(ps_t, j), tile(sum_hot[i], j),
                                                 window[0][:, i * ROW:i * ROW + P],
                                                 start=False, stop=False, skip_group_check=True)
                                last = nc.tensor.matmul(ps_x[:, j:j + 1], tile(sum_hot[i], j), ones[:, 0:1],
                                                        start=False, stop=False, skip_group_check=True)
                        last.then_inc(group_summed, 1)
                    for bank, zeros in banks:
                        last = nc.tensor.matmul(bank, ones[:], zeros, start=False, stop=True, skip_group_check=True)
                    last.then_inc(block_summed, 1)

            with is_general(pe):
                for c in range(2):
                    last = nc.tensor.transpose(ps_u[:, c * P:(c + 1) * P], weight_f[:, c, :], ident)
                last.then_inc(weight_T, 1)
                all_edges(pe, lambda *at: step(*at, rows=general_rows, gathered=general_gathered))
                pe.wait_ge(zeros_ready, 1)
                sum_by_node()
                meet(pe, 1)
                meet(pe, 2)
            walk(pe, step)

        @block.vector
        def _(dve):
            links = [0]

            def link(instruction):
                links[0] += 1
                instruction.then_inc(setup_chain, 1)
                dve.wait_ge(setup_chain, links[0])

            v = nc.vector
            v.memset(halo_i[:], int(FAR)).then_inc(pads_ready, 1)
            v.memset(next_i[:], int(FAR)).then_inc(pads_ready, 1)
            v.memset(src_i[:], 0).then_inc(pads_ready, 1)
            v.memset(weight_f[:], 0.0).then_inc(pads_ready, 1)
            v.memset(ones[:], 1.0)
            v.memset(ones_bf[:], 1.0)
            v.memset(pad_rows[:, 0:P], 0.0)
            v.memset(pad_rows[:, P:ROW], FAR)
            v.memset(count[:], 1.0)
            v.memset(bias_in[:, 0, P:ROW], 0.0)
            dve.wait_ge(pads_ready, 4)
            dve.wait_ge(edges_loaded, 16 * 18)
            v.tensor_copy(src_f[:], src_i[:]).then_inc(table_in, 1)
            v.tensor_copy(first_next[:], next_i[:])
            link(v.tensor_copy(halo[:], halo_i[:]))
            here = halo[:, :, REACH:REACH + P]
            v.scalar_tensor_tensor(dst_idx_f[:], here, FAR, here, ALU.is_lt, ALU.mult).then_inc(table_in, 1)
            v.tensor_copy(first[:], halo[:, :, REACH:REACH + 1].rearrange("p c a -> p (c a)")).then_inc(table_in, 1)
            for i in range(2):
                dve.wait_ge(table_T, i + 1)
                v.tensor_copy(gather_idx[:, :, i * T:(i + 1) * T],
                              (ps_t[:, 0:ET], ps_u[:, 512:512 + ET])[i].rearrange("p (g t) -> p g t", t=T)).then_inc(idx_ready, 1)
            for d in range(1, REACH + 1):
                link(v.tensor_tensor(same[:, :, 0:P + d], halo[:, :, REACH - d:REACH + P],
                                     halo[:, :, REACH:REACH + P + d], ALU.is_equal))
                link(v.tensor_tensor(count[:], count[:], same[:, :, d:d + P], ALU.add))
                link(v.tensor_tensor(count[:], count[:], same[:, :, 0:P], ALU.add))
            link(v.tensor_scalar(recip[:], count[:], COUNT_EPS, None, ALU.add))
            link(v.reciprocal(recip[:], recip[:]))
            link(v.scalar_tensor_tensor(recip[:], count[:], 0.0, recip[:], ALU.is_gt, ALU.mult))
            v.tensor_tensor(mean_weight[:], weight_f[:], recip[:], ALU.mult).then_inc(table_in, 1)
            dve.wait_ge(table_T, 4)
            v.tensor_copy(dst_col[:], ps_u[:, 0:ET])
            link(v.tensor_copy(weight_col[:], ps_u[:, 256:256 + ET]))
            dve.wait_ge(loaded, 16 * 10)
            dve.wait_ge(consts_loaded, 16)
            link(v.tensor_reduce(w_mean[:], weights[:], AX.X, ALU.add))
            link(v.tensor_scalar(w_mean[:], w_mean[:], -1.0 / P, None, ALU.mult))
            for i, centred in enumerate((w_src, w_dst, u_x_gate[:, 0:P], u_msg)):
                link(v.tensor_scalar(centred, weights[:, i], w_mean[:, i:i + 1], None, ALU.add))
            link(v.tensor_reduce(bias_mean[:], bias_in[:, :, 0:P], AX.X, ALU.add))
            link(v.tensor_scalar(bias_mean[:], bias_mean[:], -1.0 / P, None, ALU.mult))
            for i in range(2):
                link(v.tensor_scalar(bias_left[:, 0, i, 0:P], bias_in[:, i, 0:P], bias_mean[:, i:i + 1], None, ALU.add))
            link(v.tensor_copy(bias_left[:, 0, :, P:ROW], bias_in[:, :, P:ROW]))
            for i in range(3):
                link(v.tensor_copy(bias_part[:, i], bias_left[:, i]))
                if i < 2:
                    link(v.tensor_tensor(bias_left[:, i + 1], bias_left[:, i], bias_part[:, i], ALU.subtract))
            mask = [const_in[:, C_PART + i:C_PART + i + 1] for i in range(3)]
            link(v.tensor_scalar(bias_sum[:, 0], bias_part[:, 0], mask[0], None, ALU.mult))
            for i in (1, 2):
                link(v.scalar_tensor_tensor(bias_sum[:, i], bias_part[:, i], mask[i], bias_sum[:, i - 1],
                                            ALU.mult, ALU.add))
            for j in range(T):
                v.tensor_copy(msg_bias[:, j], bias_sum[:, 2, 0, 0:P])
            for j in range(2):
                last = v.tensor_copy(upd_bias[:, j], bias_sum[:, 2, 1])
            last.then_inc(params_ready, 1)

            v.tensor_copy(sel_rhs[:, :, 0:P], here)
            v.tensor_copy(sel_rhs[:, :, P:ROW], const_in[:, C_TBASE:C_TBASE + 2].unsqueeze(2))
            link(v.memset(first[0:1, 0:1], -1.0))
            bound = const_in[:, C_BOUND:C_BOUND + 2 * T * P]
            for c in range(2):
                link(v.tensor_scalar(sel[:, c], bound, first_next[:, c:c + 1], None, ALU.is_le))
                last = v.scalar_tensor_tensor(sel[:, c], bound, first[:, c:c + 1], sel[:, c], ALU.is_gt, ALU.mult)
            last.then_inc(sel_ready, 1)
            dve.wait_ge(sel_done, 1)
            banks = [ps_xs, ps_xd, ps_z, ps_h]
            for n in range(2 * T):
                link(v.tensor_scalar(fine_out[:], banks[n // 2][:, n % 2 * ROW:n % 2 * ROW + P],
                                     const_in[:, C_BOUNDC + n:C_BOUNDC + n + 1], None, ALU.is_lt, ALU.add,
                                     accum_out=fine[:, n:n + 1]))
            for n in range(2 * T):
                link(v.tensor_tensor(starts[:, n:n + 1], banks[n // 2][:, n % 2 * ROW + P:(n % 2 + 1) * ROW],
                                     fine[:, n:n + 1], ALU.add))
            v.tensor_tensor(odd[:, 0], here, halo[:, :, REACH + 1:REACH + 1 + P], ALU.is_gt)
            link(v.tensor_tensor(odd[:, 1], here, halo[:, :, 2 * REACH:2 * REACH + P], ALU.is_equal))
            link(v.scalar_tensor_tensor(odd[:, 1], here, FAR, odd[:, 1], ALU.is_lt, ALU.mult))
            steps = const_in[:, C_WIN:C_WIN + T]
            v.tensor_tensor(ends[:], starts[:, T:2 * T], steps, ALU.subtract)
            link(v.tensor_tensor(starts[:, 0:T], starts[:, 0:T], steps, ALU.subtract))
            link(v.tensor_reduce(block_start[:], starts[:, 0:T], AX.X, ALU.min))
            v.memset(odd[:, 2], 0.0)
            link(v.tensor_scalar(ends[:], ends[:], float(P), block_start[:], ALU.subtract, ALU.is_gt))
            v.tensor_copy(odd[0:NB, 2, 0, 0:T], ends[0:NB])
            link(v.tensor_tensor(odd[0:NB, 2, 1, 0:1], block_start[0:NB], const_in[0:NB, C_LIMIT:C_LIMIT + 1],
                                 ALU.is_gt))
            v.tensor_reduce(odd_sum[:], odd[:].rearrange("p a b c -> p (a b c)"), AX.X, ALU.add).then_inc(odd_ready, 1)
            v.tensor_scalar(block_start[:], block_start[:], float(EDGE0), None, ALU.add).then_inc(
                block_starts_ready, 1)
            dve.wait_ge(odd_done, 1)
            link(v.tensor_scalar(general[:], ps_x[:, 0:1], 1.0, None, ALU.min))
            v.tensor_copy(general_i[:], general[:])
            dve.wait_ge(starts_T, 1)
            v.tensor_copy(start_row[:], ps_t[0:1, 0:P]).then_inc(starts_ready, 1)

            def by_row(column):
                return column.unsqueeze(2).to_broadcast([P, T, P])

            def z_norm(g, gh, gs):
                dve.wait_ge(z_rstd_ready, g + 1)
                wait(dve, e3_done, g)
                v.tensor_tensor(tiles(zn[:]), tiles(ps_z[:]), by_row(z_rstd[:]), ALU.mult).then_inc(zn_ready, 1)

            def rows(g, gh, gs):
                dve.wait_ge(e4_done, g + 1)
                wait(dve, rows_stored[gs], 16 * gh)
                r = msg_rows[gs][:].rearrange("p (j h) -> p j h", h=ROW)
                v.tensor_tensor(r[:, :, 0:P], tiles(ps_z[:]), by_row(weight_col[:, bass.ds(g * T, T)]), ALU.mult)
                v.tensor_copy(r[:, :, P:ROW], dst_col[:, bass.ds(g * T, T)].unsqueeze(2)).then_inc(rows_ready, 1)

            def dst_places(q, b, kh, ks):
                dve.wait_ge(win_loaded[2 * ks + b], 16 * 2 * (kh + 1))
                w = window[2 * ks + b][:].rearrange("p (j h) -> p j h", h=ROW)
                v.tensor_tensor(dst_place[b][:].unsqueeze(2), w[:, :, P:ROW],
                                tile_base[:, bass.ds(q * T, T)].unsqueeze(2), ALU.subtract).then_inc(place_chain, 1)

            def one_hots(q, b, kh, ks):
                dve.wait_ge(place_chain, q + 1)
                wait(dve, n2_done, 2 * q - 2)
                v.tensor_tensor(tiles(onehot[b][:]), iota_row.unsqueeze(1).to_broadcast([P, T, P]),
                                by_row(dst_place[b][:]), ALU.is_equal).then_inc(hot_ready, 1)

            def residual(q, b, kh, ks):
                gates = gate_small[b]
                dve.wait_ge(gate_chain, 2 * q + 2)
                v.scalar_tensor_tensor(gates[:, 2], gates[:, 1], 2.0, gates[:, 1], ALU.add, ALU.mult).then_inc(
                    y_chain, 1)
                dve.wait_ge(n4_done, q + 1)
                for j in range(T):
                    cols = slice(j * P, (j + 1) * P)
                    last = v.scalar_tensor_tensor(y[b][:, cols], ps_h[:, cols], gates[:, 1, j:j + 1],
                                                  x_rows[2 * ks + b][:, cols], ALU.mult, ALU.add)
                last.then_inc(y_ready, 1)

            def y_halves(q, b, kh, ks):
                dve.wait_ge(y_ready, q + 1)
                for j in range(T):
                    last = v.bn_stats(y_stats[b][:, j], y[b][:, j * P:(j + 1) * P])
                last.then_inc(y_chain, 1)

            def small_sums(y_block, gate_block):
                if gate_block is not None:
                    n, c = gate_block[:2]
                    dve.wait_ge(gate_exp_ready, n + 1)
                    v.tensor_scalar(gate_small[c][:, 0], gate_exp[c][:], 2.0, 1.0, ALU.mult, ALU.add).then_inc(
                        gate_chain, 1)
                if y_block is not None:
                    q, b = y_block[:2]
                    stats, small = y_stats[b], y_small[b]
                    dve.wait_ge(y_chain, 4 * q + 2)
                    v.tensor_tensor(small[:, 0], stats[:, :, 1], stats[:, :, 4], ALU.subtract)
                    v.scalar_tensor_tensor(small[:, 1], gate_small[b][:, 2], P * LN_EPS / 4, stats[:, :, 2],
                                           ALU.mult, ALU.add).then_inc(y_chain, 1)
                if gate_block is not None:
                    dve.wait_ge(gate_chain, 2 * n + 1)
                    v.reciprocal(gate_small[c][:, 1], gate_small[c][:, 0]).then_inc(gate_chain, 1)
                if y_block is not None:
                    dve.wait_ge(y_chain, 4 * q + 3)
                    v.scalar_tensor_tensor(small[:, 2], small[:, 0], P / 4.0, small[:, 0], ALU.mult, ALU.mult)
                    v.tensor_tensor(small[:, 3], small[:, 1], stats[:, :, 5], ALU.add).then_inc(y_chain, 1)
                    v.scalar_tensor_tensor(small[:, 5], small[:, 0], -0.5, stats[:, :, 1],
                                           ALU.mult, ALU.add).then_inc(y_mean_ready, 1)
                    dve.wait_ge(y_chain, 4 * q + 4)
                    v.tensor_tensor(small[:, 4], small[:, 2], small[:, 3], ALU.add).then_inc(y_var_ready, 1)

            def result(q, b, kh, ks):
                dve.wait_ge(y_rstd_ready, q + 1)
                dve.wait_ge(y_mean_ready, q + 1)
                wait(dve, out_stored[b], 16 * (2 * kh + ks))
                for j in range(T):
                    cols = slice(j * P, (j + 1) * P)
                    last = v.tensor_scalar(out_rows[b][:, cols], y[b][:, cols], y_small[b][:, 5, j:j + 1],
                                           y_rstd[b][:, j:j + 1], ALU.subtract, ALU.mult)
                last.then_inc(out_ready, 1)

            def step(g, gh, gs, k, kh, ks):
                this, former = group(g, gh, gs, 0), group(g, gh, gs, 1)
                for b in range(2):
                    at = [behind(k, kh, ks, b, n) if k is not None else None for n in range(4)]
                    on(dst_places, at[0])
                    on(one_hots, at[0])
                    on(result, at[3])
                    on(residual, at[2])
                    on(y_halves, at[2])
                    on(*((rows, former) if b == 0 else (z_norm, this)))
                    small_sums(at[2], at[1])

            def sum_by_node():
                v.memset(xT[0][:], 0.0).then_inc(zeros_ready, 1)
                for j in range(T):
                    v.tensor_scalar(block_nodes[:, j * P:(j + 1) * P], iota_row, float(j * P), None, ALU.add)
                    last = v.tensor_scalar(node_col[:, j:j + 1], const_in[:, C_TBASE:C_TBASE + 1], 1.0 / P,
                                           float(j * P), ALU.mult, ALU.add)
                last.then_inc(sum_chain, 1)
                with dve.Fori(0, NB) as q:
                    with dve.Fori(0, EG) as g:
                        dve.wait_ge(sum_chain, 5 * q + 1)
                        dve.wait_ge(group_loaded, q * (16 * EG) + g * 16 + 16)
                        for i in range(T):
                            last = v.tensor_scalar(sum_hot[i][:], block_nodes[:],
                                                   window[0][:, i * ROW + P:(i + 1) * ROW], None, ALU.is_equal)
                        last.then_inc(group_hot, 1)
                    dve.wait_ge(block_summed, q + 1)
                    dve.wait_ge(sums_stored, q * 16 + 16)
                    v.tensor_scalar(node_recip[:, 0], ps_x[:, 0:T], COUNT_EPS, None, ALU.add).then_inc(sum_chain, 1)
                    dve.wait_ge(sum_chain, 5 * q + 2)
                    v.reciprocal(node_recip[:, 1], node_recip[:, 0]).then_inc(sum_chain, 1)
                    dve.wait_ge(sum_chain, 5 * q + 3)
                    v.scalar_tensor_tensor(node_recip[:, 2], ps_x[:, 0:T], 0.0, node_recip[:, 1],
                                           ALU.is_gt, ALU.mult).then_inc(sum_chain, 1)
                    dve.wait_ge(sum_chain, 5 * q + 4)
                    r = msg_rows[0][:].rearrange("p (j h) -> p j h", h=ROW)
                    v.tensor_tensor(r[:, :, 0:P], tiles(ps_t[:]), by_row(node_recip[:, 2]), ALU.mult).then_inc(
                        sums_read, 1)
                    v.tensor_copy(r[:, :, P:ROW], node_col[:].unsqueeze(2)).then_inc(sums_ready, 1)
                    v.tensor_scalar(block_nodes[:], block_nodes[:], float(BN), None, ALU.add).then_inc(sum_chain, 1)
                    dve.wait_ge(sums_ready, q + 1)
                    v.tensor_scalar(node_col[:], node_col[:], float(BN), None, ALU.add).then_inc(sum_chain, 1)

            with is_general(dve):
                dve.wait_ge(weight_T, 1)
                link(v.tensor_copy(weight_col[:], ps_u[:, 0:ET]))
                all_edges(dve, step)
                sum_by_node()
                meet(dve, 1)
                meet(dve, 2)
            walk(dve, step)


def constants(n_nodes):
    blocks = -(-n_nodes // (T * P))
    wt = blocks * T
    at = const_columns(wt)
    c = np.zeros((P, at[-1]), np.float32)
    rows = np.arange(P, dtype=np.float32)
    firsts = np.concatenate([min(q * T * P, n_nodes - T * P) + P * np.arange(T) for q in range(blocks)])
    by_tile = np.zeros((2, T, P))
    by_tile[0, :, :blocks] = firsts.reshape(blocks, T).T
    by_tile[1, :, :blocks] = by_tile[0, :, :blocks] + P
    by_tile = by_tile.reshape(2 * T, P)
    pair = np.arange(P) // 2
    limit = np.where(pair + 2 >= blocks // 2, float(n_nodes), (pair + 2) * T * P - SPAN)
    c[:, at[0]:at[1]] = np.eye(P)
    c[:, at[1]:at[2]] = rows[None, :]
    c[:, at[2]:at[3]] = by_tile.reshape(1, -1)
    c[:, at[3]:at[4]] = by_tile.T
    c[:, at[4]] = rows * P
    c[:, at[4] + 1] = (rows + P) * P
    c[:, at[5]:at[6]] = firsts[None, :]
    c[:, at[6]:at[7]] = np.eye(P)[:, :3]
    c[:, at[7]] = limit
    c[:, at[8]:at[9]] = HALF * np.arange(T)[None, :]
    return c


_INS = ["x", "src", "dst", "edge_weight", "L0_gnn_msg_w", "L0_gnn_msg_b", "L0_gnn_msg_g", "L0_gnn_msg_beta",
        "L0_gnn_upd_w", "L0_gnn_upd_b", "L0_gnn_upd_g", "L0_gnn_upd_beta", "L0_gnn_gate_w", "L0_gnn_gate_b"]


def kernel(**inputs):
    import concourse.bacc as _bacc
    from concourse.bass_utils import run_bass_kernel_spmd as _run

    nc = _bacc.Bacc("TRN2", target_bir_lowering=False, num_devices=1)
    arrays, args = {}, []
    given = [(name, np.ascontiguousarray(inputs[name])) for name in _INS]
    given.append(("constants", constants(inputs["x"].shape[0])))
    for name, a in given:
        arrays[f"in_{name}"] = a
        args.append(nc.dram_tensor(f"in_{name}", a.shape, mybir.dt.from_np(a.dtype), kind="ExternalInput").ap())
    args.append(nc.dram_tensor("out_0", inputs["x"].shape, F32, kind="ExternalOutput").ap())
    gnn_kernel(nc, *args)
    r = _run(nc, [arrays], core_ids=[0])
    return r.results[0]["out_0"]
```

```python
from contextlib import ExitStack

import concourse.bass as bass
import numpy as np
from concourse import mybir

ALU = mybir.AluOpType
ACT = mybir.ActivationFunctionType
AX = mybir.AxisListType
F32 = mybir.dt.float32
I32 = mybir.dt.int32
BF16 = mybir.dt.bfloat16

P = 128
T = 4
LN_EPS = 1e-05
COUNT_EPS = 1e-08
REACH = 9
HALF = P // 2
SPAN = (T - 1) * HALF + P
FAR = float(1 << 20)
LN_EXP_SET = 6
LAG = 3
ROW = P + 1


def tiles(ap):
    return ap.rearrange("p (t h) -> p t h", h=P)


def const_columns(wt):
    sizes = [P, P, 2 * T * P, 2 * T, 2, wt, 3, 1, T]
    return [sum(sizes[:i]) for i in range(len(sizes) + 1)]


def gnn_kernel(nc, x, src, dst, edge_weight, msg_w, msg_b, msg_g, msg_beta,
               upd_w, upd_b, upd_g, upd_beta, gate_w, gate_b, consts, out):
    N, H = x.shape
    E, = src.shape
    ET = -(-E // P)
    EG = -(-ET // T)
    assert H == P and ET == EG * T and P < ET <= 2 * P
    BN = T * P
    NB = -(-N // BN)
    NK = NB // 2
    assert NB == 2 * NK and NK == EG and EG % 2 == 1
    WT = NB * T
    LAST = N - BN
    assert 2 * E == N
    EDGE0 = -(-(T - 1) * HALF // P) * P
    PAD0 = EDGE0 + EG * BN
    MSG0 = PAD0 + -(-SPAN // P) * P
    C_IDENT, C_IOTA, C_BOUND, C_BOUNDC, C_TBASE, C_TILE, C_PART, C_LIMIT, C_WIN, C_END = const_columns(WT)

    with ExitStack() as ctx:
        def sb(name, shape, dt=F32):
            return ctx.enter_context(nc.sbuf_tensor(name, shape, dt))

        def psum(name):
            return ctx.enter_context(nc.psum_tensor(name, [P, 512], F32))

        def sem(name):
            return ctx.enter_context(nc.semaphore(name))

        rows_dram = nc.dram_tensor("rows_scratch", [MSG0 + NB * BN, ROW], F32, kind="Internal").ap()

        const_in = sb("const_in", [P, C_END])
        ident = const_in[:, C_IDENT:C_IDENT + P]
        iota_row = const_in[:, C_IOTA:C_IOTA + P]
        tile_base = const_in[:, C_TILE:C_TILE + WT]
        ones = sb("ones", [P, P])
        ones_bf = sb("ones_bf", [P, P], BF16)
        weights = sb("weights", [P, 4, P])
        w_src, w_dst, u_msg = weights[:, 0], weights[:, 1], weights[:, 3]
        u_x_gate = sb("u_x_gate", [P, ROW])
        msg_bias, upd_bias = sb("msg_bias", [P, T, P], BF16), sb("upd_bias", [P, 2, ROW], BF16)
        columns = sb("columns", [P, 4])
        gather_idx = sb("gather_idx", [P, EG, 2 * T], I32)
        dst_col = sb("dst_col", [P, ET])
        weight_col = sb("weight_col", [P, ET])
        start_row = sb("start_row", [1, P], I32)

        idx_slot = [sb(f"idx_slot{s}", [P, 2 * T], I32) for s in range(2)]
        pair_rows = [sb(f"pair_rows{s}", [P, 2 * T * P]) for s in range(2)]
        xsT = sb("xsT", [P, 512])
        xdT = sb("xdT", [P, 512])
        squares = sb("squares", [P, 3, 512])
        z_square = sb("z_square", [P, T])
        z_ln = sb("z_ln", [P, T])
        z_rstd = sb("z_rstd", [P, T])
        zn = sb("zn", [P, 512])
        emT = sb("emT", [P, 512])
        msg_rows = [sb(f"msg_rows{s}", [P, T * ROW]) for s in range(2)]

        x_rows = [sb(f"x_rows{s}", [P, 512]) for s in range(4)]
        window = [sb(f"window{s}", [P, T * ROW]) for s in range(4)]
        xT = [sb(f"xT{s}", [P, 512]) for s in range(2)]
        onehot = [sb(f"onehot{s}", [P, 512]) for s in range(2)]
        u_square = [sb(f"u_square{s}", [P, T]) for s in range(2)]
        u_ln = [sb(f"u_ln{s}", [P, T]) for s in range(2)]
        u_rstd = [sb(f"u_rstd{s}", [P, T]) for s in range(2)]
        gate_exp = [sb(f"gate_exp{s}", [P, T]) for s in range(2)]
        gate_small = [sb(f"gate_small{s}", [P, 3, T]) for s in range(2)]
        dst_place = [sb(f"dst_place{s}", [P, T]) for s in range(2)]
        un = [sb(f"un{s}", [P, 512]) for s in range(2)]
        hT = [sb(f"hT{s}", [P, 512]) for s in range(2)]
        y = [sb(f"y{s}", [P, 512]) for s in range(2)]
        y_stats = [sb(f"y_stats{s}", [P, T, 6]) for s in range(2)]
        y_small = [sb(f"y_small{s}", [P, 6, T]) for s in range(2)]
        y_ln = [sb(f"y_ln{s}", [P, T]) for s in range(2)]
        y_rstd = [sb(f"y_rstd{s}", [P, T]) for s in range(2)]
        out_rows = [sb(f"out_rows{s}", [P, 512]) for s in range(2)]

        general_rows = [sb(f"general_rows{s}", [P, 2 * T * P]) for s in range(2)]
        sum_hot = [onehot[0], onehot[1], un[0], un[1]]
        block_nodes = sb("block_nodes", [P, 512])
        node_col = sb("node_col", [P, T])
        node_recip = sb("node_recip", [P, 3, T])

        ps_xs = psum("ps_xs")
        ps_xd = psum("ps_xd")
        ps_z = psum("ps_z")
        ps_x = psum("ps_x")
        ps_t = psum("ps_t")
        ps_u = ctx.enter_context(nc.psum_tensor("ps_u", [P, 1024], F32))
        ps_h = psum("ps_h")

        def sel_out(n):
            return (ps_h, ps_x, ps_t)[n // 3][:, n % 3 * ROW:(n % 3 + 1) * ROW]

        def u_tile(j, n):
            return ps_u[:, (j // 2) * 512 + (j % 2) * ROW:][:, 0:n]

        u_by_bank = ps_u[:].rearrange("p (a c) -> p a c", a=2)[:, :, 0:2 * ROW].rearrange(
            "p a (t h) -> p a t h", h=ROW)
        u_gates = u_by_bank[:, :, :, P:ROW]

        w_mean = sb("w_mean", [P, 4])
        bias_in = sb("bias_in", [P, 2, ROW])
        bias_mean = sb("bias_mean", [P, 2])
        bias_left = sb("bias_left", [P, 3, 2, ROW])
        bias_part = sb("bias_part", [P, 3, 2, ROW], BF16)
        bias_sum = sb("bias_sum", [P, 3, 2, ROW])
        halo_i = sb("halo_i", [P, 2, P + 2 * REACH], I32)
        halo = sb("halo", [P, 2, P + 2 * REACH])
        next_i = sb("next_i", [P, 2], I32)
        first_next = sb("first_next", [P, 2])
        first = sb("first", [P, 2])
        src_i = sb("src_i", [P, 2, P], I32)
        src_f = sb("src_f", [P, 2, P])
        dst_idx_f = sb("dst_idx_f", [P, 2, P])
        weight_f = sb("weight_f", [P, 2, P])
        mean_weight = sb("mean_weight", [P, 2, P])
        same = [sb(f"same{s}", [P, 2, P + REACH], BF16) for s in range(3)]
        count_side = [sb(f"count_side{s}", [P, 2, P], BF16) for s in range(2)]
        count = sb("count", [P, 2, P])
        recip = sb("recip", [P, 2, P])
        odd = sb("odd", [P, 3, 2, P])
        odd_sum = sb("odd_sum", [P, 1])
        sel = sb("sel", [P, 2, 2 * T * P])
        sel_rhs = sb("sel_rhs", [P, 2, ROW])
        fine = sb("fine", [P, 2 * T])
        fine_out = sb("fine_out", [P, 2 * T, P])
        starts = sb("starts", [P, 2 * T])
        ends = sb("ends", [P, T])
        block_start = sb("block_start", [P, 1])
        general = sb("general", [P, 1])
        general_i = sb("general_i", [P, 1], I32)
        pad_rows = sb("pad_rows", [P, ROW])

        loaded, edges_loaded, consts_loaded = sem("loaded"), sem("edges_loaded"), sem("consts_loaded")
        pads_ready = sem("pads_ready")
        table_in, table_T = sem("table_in"), sem("table_T")
        keys_loaded = sem("keys_loaded")
        setup_chain, count_chain = sem("setup_chain"), sem("count_chain")
        sel_ready, sel_done = sem("sel_ready"), sem("sel_done")
        odd_ready, odd_done = sem("odd_ready"), sem("odd_done")
        idx_ready, params_ready = sem("idx_ready"), sem("params_ready")
        block_starts_ready, starts_T, starts_ready = sem("block_starts_ready"), sem("starts_T"), sem("starts_ready")
        pads_stored = sem("pads_stored")
        met, weight_T, zeros_ready, sum_chain = sem("met"), sem("weight_T"), sem("zeros_ready"), sem("sum_chain")
        general_copied, general_gathered = sem("general_copied"), [sem(f"general_gathered{s}") for s in range(2)]
        group_loaded, group_hot, group_summed = sem("group_loaded"), sem("group_hot"), sem("group_summed")
        block_summed, sums_read, sums_ready, sums_stored = (
            sem("block_summed"), sem("sums_read"), sem("sums_ready"), sem("sums_stored"))

        walk_sems = []

        def walk_sem(name):
            walk_sems.append(sem(name))
            return walk_sems[-1]

        slot_copied, slot_seen = sem("slot_copied"), sem("slot_seen")
        gathered = [sem(f"gathered{s}") for s in range(2)]
        rows_stored = [walk_sem(f"rows_stored{s}") for s in range(2)]
        x_loaded = [walk_sem(f"x_loaded{s}") for s in range(4)]
        win_loaded = [walk_sem(f"win_loaded{s}") for s in range(4)]
        out_stored = [walk_sem(f"out_stored{s}") for s in range(2)]
        e1_done, e2_done, e3_done, e4_done = (walk_sem(f"e{i}_done") for i in (1, 2, 3, 4))
        n1_done, n2_done, n3_done, n4_done = (walk_sem(f"n{i}_done") for i in (1, 2, 3, 4))
        pairT_ready, z_ln_ready, z_rstd_ready, emT_ready = (
            walk_sem("pairT_ready"), walk_sem("z_ln_ready"), walk_sem("z_rstd_ready"), walk_sem("emT_ready"))
        gate_exp_ready = walk_sem("gate_exp_ready")
        xT_ready, u_ln_ready, u_rstd_ready, hT_ready, y_ln_ready, y_rstd_ready = (
            walk_sem("xT_ready"), walk_sem("u_ln_ready"), walk_sem("u_rstd_ready"), walk_sem("hT_ready"),
            walk_sem("y_ln_ready"), walk_sem("y_rstd_ready"))
        zn_ready, rows_ready = walk_sem("zn_ready"), walk_sem("rows_ready")
        hot_ready, un_ready, y_ready, y_var_ready, out_ready = (
            walk_sem("hot_ready"), walk_sem("un_ready"), walk_sem("y_ready"),
            walk_sem("y_var_ready"), walk_sem("out_ready"))
        y_mean_ready = walk_sem("y_mean_ready")
        place_chain, gate_chain, y_chain = walk_sem("place_chain"), walk_sem("gate_chain"), walk_sem("y_chain")
        z_square_ready, u_square_ready = walk_sem("z_square_ready"), walk_sem("u_square_ready")

        def wait(eng, semaphore, value):
            if not (isinstance(value, int) and value <= 0):
                eng.wait_ge(semaphore, value)

        def head(eng, step, between=()):
            for g in range(LAG):
                step(g, g // 2, g % 2, None, None, None)
                for task in between[g:g + 1]:
                    task()

        def rest(eng, step):
            for k in range(2):
                step(k + LAG, (k + LAG) // 2, (k + LAG) % 2, k, 0, k)
            with eng.Fori(1, (NK - LAG) // 2) as m:
                for ks in range(2):
                    step(2 * m + (ks + LAG), m + (ks + LAG) // 2, (ks + LAG) % 2, 2 * m + ks, m, ks)
            for k in range(NK - LAG, NK + 2):
                g = k + LAG
                step(*((g, g // 2, g % 2) if g == EG else (None, None, None)), k, k // 2, k % 2)

        def all_edges(eng, step):
            for g in range(3):
                step(g, g // 2, g % 2, None, None, None)
            with eng.Fori(1, EG // 2) as m:
                for s in range(2):
                    step(2 * m + (s + 1), m + (s + 1) // 2, (s + 1) % 2, None, None, None)
            step(EG, EG // 2, EG % 2, None, None, None)

        def meet(eng, n):
            eng.drain().then_inc(met, 1)
            eng.wait_ge(met, 5 * n)
            eng.drain()

        def restart(eng, n):
            meet(eng, 2 * n - 1)
            if eng is nc.sync:
                for s in walk_sems:
                    eng.sem_clear(s)
            meet(eng, 2 * n)

        def is_general(eng):
            eng.wait_ge(starts_ready, 1)
            return eng.If(eng.value_load(general_i[0:1, 0:1], min_val=0, max_val=1) > 0)

        def behind(k, kh, ks, b, n):
            d = (b - n) // 2
            q = 2 * (k + d) + (b - n) % 2
            if isinstance(q, int) and not 0 <= q < NB:
                return None
            return q, (b - n) % 2, kh + (ks + d) // 2, (ks + d) % 2

        def group(g, gh, gs, n):
            if g is None or (isinstance(g, int) and not 0 <= g - n < EG):
                return None
            return g - n, gh + (gs - n) // 2, (gs - n) % 2

        def on(task, block):
            if block is not None:
                task(*block)

        assert (NK - LAG) % 2 == 0
        block = ctx.enter_context(nc.Block())

        @block.sync
        def _(sp):
            full, over = ET - P - 1, E - (ET - 1) * P
            by_tile = dst[0:(ET - 1) * P].rearrange("(t q) -> t q", q=P)
            before = dst[P - REACH:P - REACH + (ET - 2) * P].rearrange("(t q) -> t q", q=P)[:, 0:REACH]
            after = dst[P:(ET - 1) * P].rearrange("(t q) -> t q", q=P)[:, 0:REACH]

            def row(v, a, n):
                return v[a:a + n].rearrange("(a q) -> a q", a=1)

            def spread(v, buffer, semaphore):
                v2 = v[0:(ET - 1) * P].rearrange("(t q) -> t q", q=P)
                sp.dma_start(buffer[:, 0, :], v2[0:P]).then_inc(semaphore, 16)
                sp.dma_start(buffer[0:full, 1, :], v2[P:]).then_inc(semaphore, 16)
                sp.dma_start(buffer[full:full + 1, 1, 0:over], row(v, (ET - 1) * P, over)).then_inc(semaphore, 16)

            sp.dma_start(const_in[:], consts).then_inc(consts_loaded, 16)
            sp.wait_ge(pads_ready, 4)
            spread(src, src_i, keys_loaded)
            spread(dst, halo_i[:, :, REACH:REACH + P], keys_loaded)
            with nc.allow_non_contiguous_dma(reason="a word for each tile"):
                for a, b in ((next_i[:, 0:1], after[0:P, 0:1]),
                             (next_i[0:full - 1, 1:2], after[P:, 0:1]),
                             (next_i[full - 1:full, 1:2], row(dst, (ET - 1) * P, 1)),
                             (halo_i[1:P, 0, 0:REACH], before[0:P - 1]),
                             (halo_i[0:full, 1, 0:REACH], before[P - 1:]),
                             (halo_i[full:full + 1, 1, 0:REACH], row(dst, (ET - 1) * P - REACH, REACH)),
                             (halo_i[:, 0, REACH + P:], after[0:P]),
                             (halo_i[0:full - 1, 1, REACH + P:], after[P:]),
                             (halo_i[full - 1:full, 1, REACH + P:], row(dst, (ET - 1) * P, REACH))):
                    sp.dma_start(a, b).then_inc(edges_loaded, 16)
            spread(edge_weight, weight_f, edges_loaded)
            sp.wait_ge(params_ready, 1)
            pads = [*range(0, EDGE0, P), *range(PAD0, MSG0, P)]
            for a in pads:
                sp.dma_start(rows_dram[a:a + P, :], pad_rows[:]).then_inc(pads_stored, 16)
            sp.wait_ge(pads_stored, 16 * len(pads))

            def block_rows(t, q, half=None):
                first_row = LAST if isinstance(q, int) and q == NB - 1 else q * BN
                if half is None:
                    return t[bass.ds(first_row, BN), :].rearrange("(j p) h -> p j h", p=P)
                return t[bass.ds(first_row + half * (BN // 2), BN // 2), :].rearrange("(j p) h -> p j h", p=P)

            def load_x(k, ks, b):
                sp.dma_start(tiles(x_rows[2 * ks + b][:]), block_rows(x, 2 * k + b)).then_inc(
                    x_loaded[2 * ks + b], 16)

            def load_windows(k, ks):
                for b in range(2):
                    at = sp.value_load(start_row[0:1, bass.ds(2 * k + b, 1)], min_val=0, max_val=MSG0 - SPAN)
                    for i in range(2):
                        sp.dma_start(window[2 * ks + b][:].rearrange("p (a i h) -> p i a h", i=2, h=ROW)[:, i],
                                     rows_dram[bass.ds(at + i * HALF, 2 * P), :].rearrange(
                                         "(a p) h -> p a h", p=P)).then_inc(win_loaded[2 * ks + b], 16)

            def load_node_rows(k, ks):
                for b in range(2):
                    for i in range(2):
                        sp.dma_start(window[2 * ks + b][:].rearrange("p (i a h) -> p i a h", i=2, h=ROW)[:, i],
                                     block_rows(rows_dram[MSG0:], 2 * k + b, i)).then_inc(win_loaded[2 * ks + b], 16)

            def store_out(q, b, kh, ks):
                sp.wait_ge(out_ready, q + 1)
                if isinstance(q, int) and q == NB - 1:
                    sp.wait_ge(out_stored[0], 16 * NK)
                sp.dma_start(block_rows(out, q), tiles(out_rows[b][:])).then_inc(out_stored[b], 16)

            def store_rows(g, gh, gs):
                sp.wait_ge(rows_ready, g + 1)
                sp.dma_start(rows_dram[bass.ds(g * BN + EDGE0, BN), :].rearrange("(j p) h -> p j h", p=P),
                             msg_rows[gs][:].rearrange("p (j h) -> p j h", h=ROW)).then_inc(rows_stored[gs], 16)

            def load_first_pair(load_messages):
                load_x(0, 0, 0)
                load_x(0, 0, 1)
                sp.wait_ge(rows_stored[0], 16)
                sp.wait_ge(rows_stored[1], 16)
                load_messages(0, 0)

            def step(g, gh, gs, k, kh, ks, load_messages=load_windows):
                more = k is not None and not (isinstance(k, int) and k >= NK - 1)
                if k is not None:
                    on(store_out, behind(k, kh, ks, 0, 3))
                if more:
                    wait(sp, y_ready, 2 * k - 1)
                    load_x(k + 1, 1 - ks, 0)
                on(store_rows, group(g, gh, gs, 1))
                if k is not None:
                    on(store_out, behind(k, kh, ks, 1, 3))
                if more:
                    if isinstance(k, int):
                        for s in range(2):
                            sp.wait_ge(rows_stored[s], 16 * ((min(k + 3, EG) + 1 - s) // 2))
                    else:
                        sp.wait_ge(rows_stored[ks], 16 * (kh + 2))
                        sp.wait_ge(rows_stored[1 - ks], 16 * (kh + 1 + ks))
                    wait(sp, gate_exp_ready, 2 * k)
                    load_messages(k + 1, 1 - ks)
                    wait(sp, y_ready, 2 * k)
                    load_x(k + 1, 1 - ks, 1)

            def sum_by_node():
                for s in range(2):
                    sp.wait_ge(rows_stored[s], 16 * ((EG + 1 - s) // 2))
                sp.sem_inc(sums_stored, 16)
                sp.sem_inc(group_summed, 1)
                sp.sem_inc(sums_read, 1)
                with sp.Fori(0, NB) as q:
                    with sp.Fori(0, EG) as g:
                        sp.wait_ge(group_summed, q * EG + g + 1)
                        sp.dma_start(window[0][:].rearrange("p (j h) -> p j h", h=ROW),
                                     rows_dram[bass.ds(g * BN + EDGE0, BN), :].rearrange(
                                         "(j p) h -> p j h", p=P)).then_inc(group_loaded, 16)
                    sp.wait_ge(sums_ready, q + 1)
                    sp.dma_start(rows_dram[bass.ds(q * BN + MSG0, BN), :].rearrange("(j p) h -> p j h", p=P),
                                 msg_rows[0][:].rearrange("p (j h) -> p j h", h=ROW)).then_inc(sums_stored, 16)
                sp.wait_ge(sums_stored, 16 * (NB + 1))

            head(sp, step)
            with is_general(sp):
                for s in range(2):
                    sp.wait_ge(rows_stored[s], 16)
                restart(sp, 1)
                all_edges(sp, step)
                sum_by_node()
                restart(sp, 2)
                head(sp, step)
                load_first_pair(load_node_rows)
                rest(sp, lambda *at: step(*at, load_messages=load_node_rows))
            with sp.Else():
                load_first_pair(load_windows)
                rest(sp, step)
            for s in range(2):
                sp.wait_ge(out_stored[s], 16 * NK)
                sp.wait_ge(rows_stored[s], 16 * ((EG + 1 - s) // 2))

        @block.gpsimd
        def _(pool):
            def gather(g, s, before, rows, copied, gathered):
                if before is not None:
                    pool.wait_ge(e1_done, before)
                nc.gpsimd.tensor_copy(idx_slot[s][:], gather_idx[:, bass.ds(g, 1), :].rearrange(
                    "p a t -> p (a t)")).then_inc(copied, 1)
                pool.wait_ge(copied, g + 1)
                pool.sem_inc(slot_seen, 1)
                for j in range(2 * T):
                    nc.gpsimd.indirect_dma_start(
                        rows[s][:, j * P:(j + 1) * P], None, x,
                        bass.IndirectOffsetOnAxis(ap=idx_slot[s][:, j:j + 1], axis=0)).then_inc(gathered[s], 16)

            pool.wait_ge(idx_ready, 2)

            def first_gathers(*path):
                gather(0, 0, None, *path)
                gather(1, 1, None, *path)
                gather(2, 0, 1, *path)

            def other_gathers(*path):
                with nc.gpsimd.Fori(1, (EG - 1) // 2) as m:
                    for s in range(2):
                        gather(2 * m + (s + 1), (s + 1) % 2, 2 * m + s, *path)

            first_gathers(pair_rows, slot_copied, gathered)
            with is_general(pool):
                for s in range(2):
                    pool.wait_ge(gathered[s], 16 * 2 * T * (2 - s))
                restart(pool, 1)
                first_gathers(general_rows, general_copied, general_gathered)
                other_gathers(general_rows, general_copied, general_gathered)
                restart(pool, 2)
            other_gathers(pair_rows, slot_copied, gathered)

        @block.scalar
        def _(act):
            with nc.allow_non_contiguous_dma(reason="vectors of 128 as columns"):
                act.dma_start(weights[:, 0:2], msg_w.rearrange("(a k) h -> k a h", a=2)).then_inc(loaded, 16)
                act.dma_start(weights[:, 2:4], upd_w.rearrange("(a k) h -> k a h", a=2)).then_inc(loaded, 16)
                act.dma_start(u_x_gate[:, P:ROW], gate_w).then_inc(loaded, 16)
                for i, v in enumerate((msg_g, msg_beta, upd_g, upd_beta)):
                    act.dma_start(columns[:, i:i + 1], v.rearrange("(h a) -> h a", a=1)).then_inc(loaded, 16)
                act.dma_start(bias_in[:, 1, P:ROW],
                              gate_b.rearrange("(h a) -> h a", a=1).to_broadcast([P, 1])).then_inc(loaded, 16)
                for i, v in enumerate((msg_b, upd_b)):
                    act.dma_start(bias_in[:, i, 0:P], v.rearrange("(a h) -> a h", a=1).to_broadcast([P, P])).then_inc(
                        loaded, 16)

            def pairT(g, gh, gs):
                act.wait_ge(e1_done, g + 1)
                wait(act, e2_done, g)
                nc.scalar.copy(xsT[:], ps_xs[:]).then_inc(pairT_ready, 1)
                nc.scalar.copy(xdT[:], ps_xd[:]).then_inc(pairT_ready, 1)

            def z_rstd_of(g, gh, gs):
                act.wait_ge(e2_done, g + 1)
                for j in range(T):
                    last = nc.scalar.activation(squares[:, 2, j * P:(j + 1) * P], ps_z[:, j * P:(j + 1) * P],
                                                ACT.Square, accum_out=z_square[:, j:j + 1])
                last.then_inc(z_square_ready, 1)
                act.wait_ge(z_square_ready, g + 1)
                nc.scalar.activation(z_ln[:], z_square[:], ACT.Ln, bias=LN_EPS, scale=1.0 / P).then_inc(z_ln_ready, 1)
                act.wait_ge(z_ln_ready, g + 1)
                nc.scalar.activation(z_rstd[:], z_ln[:], ACT.Exp, scale=-0.5).then_inc(z_rstd_ready, 1)

            def emT_of(g, gh, gs):
                act.wait_ge(e3_done, g + 1)
                wait(act, e4_done, g)
                nc.scalar.activation(emT[:], ps_xs[:], ACT.Relu, bias=columns[:, 1:2],
                                     scale=columns[:, 0:1]).then_inc(emT_ready, 1)

            def xT_of(q, b, kh, ks):
                act.wait_ge(n1_done, q + 1)
                wait(act, n2_done, 2 * q - 2)
                nc.scalar.copy(xT[b][:], ps_x[:]).then_inc(xT_ready, 1)

            def gates_and_squares(q, b, kh, ks):
                for a in range(2):
                    act.wait_ge(n2_done, 2 * q + a + 1)
                    for j in (2 * a, 2 * a + 1):
                        last = nc.scalar.activation(squares[:, b, j * P:(j + 1) * P], u_tile(j, P), ACT.Square,
                                                    accum_out=u_square[b][:, j:j + 1])
                last.then_inc(u_square_ready, 1)
                nc.scalar.activation(gate_exp[b][:].rearrange("p (a t) -> p a t", a=2).unsqueeze(3), u_gates,
                                     ACT.Exp, scale=-1.0).then_inc(gate_exp_ready, 1)

            def rstds(y_block, u_block):
                if y_block is not None:
                    q, b = y_block[:2]
                    act.wait_ge(y_var_ready, q + 1)
                    nc.scalar.activation(y_ln[b][:], y_small[b][:, 4], ACT.Ln, bias=LN_EPS / 4,
                                         scale=1.0 / P).then_inc(y_ln_ready, 1)
                if u_block is not None:
                    q, b = u_block[:2]
                    act.wait_ge(u_square_ready, q + 1)
                    nc.scalar.activation(u_ln[b][:], u_square[b][:], ACT.Ln, bias=LN_EPS,
                                         scale=1.0 / P).then_inc(u_ln_ready, 1)
                if y_block is not None:
                    q, b = y_block[:2]
                    act.wait_ge(y_ln_ready, q + 1)
                    nc.scalar.activation(y_rstd[b][:], y_ln[b][:], ACT.Exp, scale=-0.5).then_inc(y_rstd_ready, 1)
                if u_block is not None:
                    q, b = u_block[:2]
                    act.wait_ge(u_ln_ready, q + 1)
                    nc.scalar.activation(u_rstd[b][:], u_ln[b][:], ACT.Exp, scale=-0.5).then_inc(u_rstd_ready, 1)

            def u_norm(q, b, kh, ks):
                act.wait_ge(u_rstd_ready, q + 1)
                wait(act, n3_done, q - 1)
                for a in range(2):
                    for j in (2 * a, 2 * a + 1):
                        last = nc.scalar.activation(un[b][:, j * P:(j + 1) * P], u_tile(j, P), ACT.Copy,
                                                    scale=u_rstd[b][:, j:j + 1])
                    last.then_inc(un_ready, 1)

            def hT_of(q, b, kh, ks):
                act.wait_ge(n3_done, q + 1)
                wait(act, n4_done, q - 1)
                nc.scalar.activation(hT[b][:], ps_t[:], ACT.Relu, bias=columns[:, 3:4],
                                     scale=columns[:, 2:3]).then_inc(hT_ready, 1)

            def step(g, gh, gs, k, kh, ks):
                this, former = group(g, gh, gs, 0), group(g, gh, gs, 1)
                for b in range(2):
                    at = [behind(k, kh, ks, b, n) if k is not None else None for n in range(4)]
                    on(gates_and_squares, at[1])
                    if b == 0:
                        on(hT_of, at[2])
                        rstds(at[3], at[1])
                        on(emT_of, former)
                        on(u_norm, at[1])
                        on(xT_of, at[0])
                        on(pairT, this)
                    else:
                        rstds(at[3], at[1])
                        on(hT_of, at[2])
                        on(xT_of, at[0])
                        on(u_norm, at[1])
                        on(z_rstd_of, this)

            act.add_instruction(mybir.InstLoadActFuncSet(
                name=nc.get_next_instruction_name(), engine=mybir.EngineType.Activation,
                act_func_set_id=LN_EXP_SET))
            act.wait_ge(loaded, 16 * 10)
            head(act, step)
            with is_general(act):
                restart(act, 1)
                all_edges(act, step)
                restart(act, 2)
                head(act, step)
            rest(act, step)

        @block.tensor
        def _(pe):
            def tile(t, j):
                return t[:, j * P:(j + 1) * P]

            def table_transposes(i, table, ps):
                pe.wait_ge(table_in, i + 1)
                for c in range(2):
                    last = nc.tensor.transpose(ps[:, c * P:(c + 1) * P], table[:, c, :], ident)
                last.then_inc(table_T, 1)

            pe.wait_ge(consts_loaded, 16)
            for i, (table, ps) in enumerate(((src_f, ps_t[:, 0:256]), (dst_idx_f, ps_u[:, 512:768]),
                                             (halo[:, :, REACH:REACH + P], ps_u[:, 0:256]))):
                table_transposes(i, table, ps)
            pe.wait_ge(sel_ready, 1)
            for n in range(2 * T):
                for c in range(2):
                    last = nc.tensor.matmul(sel_out(n), sel[:, c, n * P:(n + 1) * P], sel_rhs[:, c, :],
                                            start=c == 0, stop=c == 1)
            last.then_inc(sel_done, 1)
            pe.wait_ge(params_ready, 1)

            def mean_weights():
                table_transposes(3, mean_weight, ps_u[:, 256:512])

            def general_and_starts():
                pe.wait_ge(odd_ready, 1)
                nc.tensor.matmul(ps_u[:, 1023:1024], ones[:], odd_sum[:], start=True, stop=True).then_inc(odd_done, 1)
                pe.wait_ge(block_starts_ready, 1)
                nc.tensor.transpose(ps_t[0:1, 0:P], block_start[:], ident).then_inc(starts_T, 1)

            def bias(bank, rows):
                nc.tensor.matmul(bank, ones_bf[:], rows[:].rearrange("p t h -> p (t h)"),
                                 start=True, stop=False, skip_group_check=True)

            def pair_transposes(g, gh, gs, rows, gathered):
                pe.wait_ge(gathered[gs], 16 * 2 * T * (gh + 1))
                wait(pe, pairT_ready, 2 * g)
                wait(pe, emT_ready, g)
                for j in range(2 * T):
                    last = nc.tensor.transpose(tile((ps_xs, ps_xd)[j // T], j % T), tile(rows[gs], j), ident)
                last.then_inc(e1_done, 1)

            def message(g, gh, gs):
                pe.wait_ge(pairT_ready, 2 * g + 2)
                wait(pe, rows_ready, g)
                bias(ps_z[:], msg_bias)
                for j in range(T):
                    nc.tensor.matmul(tile(ps_z, j), tile(xsT, j), w_src, start=False, stop=False,
                                     skip_group_check=True)
                    last = nc.tensor.matmul(tile(ps_z, j), tile(xdT, j), w_dst, start=False, stop=True,
                                            skip_group_check=True)
                last.then_inc(e2_done, 1)

            def message_transposes(g, gh, gs):
                pe.wait_ge(zn_ready, g + 1)
                for j in range(T):
                    last = nc.tensor.transpose(tile(ps_xs, j), tile(zn, j), ident)
                last.then_inc(e3_done, 1)

            def message_update(g, gh, gs):
                pe.wait_ge(emT_ready, g + 1)
                for j in range(T):
                    last = nc.tensor.matmul(tile(ps_z, j), tile(emT, j), u_msg, start=True, stop=True)
                last.then_inc(e4_done, 1)

            def x_transposes(q, b, kh, ks):
                pe.wait_ge(x_loaded[2 * ks + b], 16 * (kh + 1))
                wait(pe, xT_ready, q)
                for j in range(T):
                    last = nc.tensor.transpose(tile(ps_x, j), tile(x_rows[2 * ks + b], j), ident)
                last.then_inc(n1_done, 1)

            def update(q, b, kh, ks):
                pe.wait_ge(xT_ready, q + 1)
                pe.wait_ge(hot_ready, q + 1)
                for a in range(2):
                    wait(pe, un_ready, 2 * q - 1 + a)
                    bias(ps_u[:, a * 512:a * 512 + 2 * ROW], upd_bias)
                    for j in (2 * a, 2 * a + 1):
                        nc.tensor.matmul(u_tile(j, ROW), tile(xT[b], j), u_x_gate[:], start=False, stop=False,
                                         skip_group_check=True)
                        last = nc.tensor.matmul(u_tile(j, P), tile(onehot[b], j),
                                                window[2 * ks + b][:, j * ROW:j * ROW + P], start=False, stop=True,
                                                skip_group_check=True)
                    last.then_inc(n2_done, 1)

            def update_transposes(q, b, kh, ks):
                pe.wait_ge(un_ready, 2 * q + 2)
                wait(pe, hT_ready, q)
                for j in range(T):
                    last = nc.tensor.transpose(tile(ps_t, j), tile(un[b], j), ident)
                last.then_inc(n3_done, 1)

            def back_transposes(q, b, kh, ks):
                pe.wait_ge(hT_ready, q + 1)
                wait(pe, y_ready, q)
                for j in range(T):
                    last = nc.tensor.transpose(tile(ps_h, j), tile(hT[b], j), ident)
                last.then_inc(n4_done, 1)

            def step(g, gh, gs, k, kh, ks, rows=pair_rows, gathered=gathered):
                this, former = group(g, gh, gs, 0), group(g, gh, gs, 1)
                for b in range(2):
                    at = [behind(k, kh, ks, b, n) if k is not None else None for n in range(4)]
                    on(update, at[1])
                    on(update_transposes, at[2])
                    if b == 0:
                        on(message_transposes, former)
                        on(back_transposes, at[2])
                        on(x_transposes, at[0])
                        if this is not None:
                            pair_transposes(*this, rows, gathered)
                        on(message_update, former)
                    else:
                        on(x_transposes, at[0])
                        on(message, this)
                        on(back_transposes, at[2])

            def sum_by_node():
                banks = (ps_t[:], xT[0][:]), (ps_x[:, 0:T], xT[0][:, 0:T])
                with pe.Fori(0, NB) as q:
                    pe.wait_ge(sums_read, q + 1)
                    for bank, zeros in banks:
                        nc.tensor.matmul(bank, ones[:], zeros, start=True, stop=False, skip_group_check=True)
                    with pe.Fori(0, EG) as g:
                        pe.wait_ge(group_hot, q * EG + g + 1)
                        for i in range(T):
                            for j in range(T):
                                nc.tensor.matmul(tile(ps_t, j), tile(sum_hot[i], j),
                                                 window[0][:, i * ROW:i * ROW + P],
                                                 start=False, stop=False, skip_group_check=True)
                                last = nc.tensor.matmul(ps_x[:, j:j + 1], tile(sum_hot[i], j), ones[:, 0:1],
                                                        start=False, stop=False, skip_group_check=True)
                        last.then_inc(group_summed, 1)
                    for bank, zeros in banks:
                        last = nc.tensor.matmul(bank, ones[:], zeros, start=False, stop=True, skip_group_check=True)
                    last.then_inc(block_summed, 1)

            head(pe, step, (mean_weights, general_and_starts))
            with is_general(pe):
                restart(pe, 1)
                for c in range(2):
                    last = nc.tensor.transpose(ps_u[:, c * P:(c + 1) * P], weight_f[:, c, :], ident)
                last.then_inc(weight_T, 1)
                all_edges(pe, lambda *at: step(*at, rows=general_rows, gathered=general_gathered))
                pe.wait_ge(zeros_ready, 1)
                sum_by_node()
                restart(pe, 2)
                head(pe, step)
            rest(pe, step)

        @block.vector
        def _(dve):
            links = [0]

            def link(instruction):
                links[0] += 1
                instruction.then_inc(setup_chain, 1)
                dve.wait_ge(setup_chain, links[0])

            v = nc.vector
            v.memset(halo_i[:], int(FAR)).then_inc(pads_ready, 1)
            v.memset(next_i[:], int(FAR)).then_inc(pads_ready, 1)
            v.memset(src_i[:], 0).then_inc(pads_ready, 1)
            v.memset(weight_f[:], 0.0).then_inc(pads_ready, 1)
            v.memset(ones[:], 1.0)
            v.memset(ones_bf[:], 1.0)
            v.memset(pad_rows[:, 0:P], 0.0)
            v.memset(pad_rows[:, P:ROW], FAR)
            v.memset(count_side[0][:], 1.0)
            v.memset(count_side[1][:], 0.0)
            v.memset(bias_in[:, 0, P:ROW], 0.0)
            dve.wait_ge(pads_ready, 4)
            dve.wait_ge(keys_loaded, 16 * 6)
            here = halo[:, :, REACH:REACH + P]
            v.tensor_copy(src_f[:], src_i[:]).then_inc(table_in, 1)
            link(v.tensor_copy(here, halo_i[:, :, REACH:REACH + P]))
            v.scalar_tensor_tensor(dst_idx_f[:], here, FAR, here, ALU.is_lt, ALU.mult).then_inc(table_in, 1)
            v.tensor_copy(first[:], halo[:, :, REACH:REACH + 1].rearrange("p c a -> p (c a)")).then_inc(table_in, 1)
            for i in range(2):
                dve.wait_ge(table_T, i + 1)
                v.tensor_copy(gather_idx[:, :, i * T:(i + 1) * T],
                              (ps_t[:, 0:ET], ps_u[:, 512:512 + ET])[i].rearrange("p (g t) -> p g t", t=T)).then_inc(
                                  idx_ready, 1)

            dve.wait_ge(loaded, 16 * 10)
            dve.wait_ge(consts_loaded, 16)
            v.tensor_reduce(bias_mean[:], bias_in[:, :, 0:P], AX.X, ALU.add)
            link(v.tensor_reduce(w_mean[:], weights[:], AX.X, ALU.add))
            v.tensor_scalar(bias_mean[:], bias_mean[:], -1.0 / P, None, ALU.mult)
            link(v.tensor_scalar(w_mean[:], w_mean[:], -1.0 / P, None, ALU.mult))
            for i in range(2):
                v.tensor_scalar(bias_left[:, 0, i, 0:P], bias_in[:, i, 0:P], bias_mean[:, i:i + 1], None, ALU.add)
            v.tensor_copy(bias_left[:, 0, :, P:ROW], bias_in[:, :, P:ROW])
            for i, centred in enumerate((w_src, w_dst, u_x_gate[:, 0:P], u_msg)):
                last = v.tensor_scalar(centred, weights[:, i], w_mean[:, i:i + 1], None, ALU.add)
            link(last)
            for i in range(3):
                link(v.tensor_copy(bias_part[:, i], bias_left[:, i]))
                if i < 2:
                    link(v.tensor_tensor(bias_left[:, i + 1], bias_left[:, i], bias_part[:, i], ALU.subtract))
            mask = [const_in[:, C_PART + i:C_PART + i + 1] for i in range(3)]
            link(v.tensor_scalar(bias_sum[:, 0], bias_part[:, 0], mask[0], None, ALU.mult))
            for i in (1, 2):
                link(v.scalar_tensor_tensor(bias_sum[:, i], bias_part[:, i], mask[i], bias_sum[:, i - 1],
                                            ALU.mult, ALU.add))
            for j in range(T):
                v.tensor_copy(msg_bias[:, j], bias_sum[:, 2, 0, 0:P])
            for j in range(2):
                last = v.tensor_copy(upd_bias[:, j], bias_sum[:, 2, 1])
            last.then_inc(params_ready, 1)

            dve.wait_ge(edges_loaded, 16 * 12)
            v.tensor_copy(first_next[:], next_i[:])
            v.tensor_copy(sel_rhs[:, :, 0:P], here)
            v.tensor_copy(sel_rhs[:, :, P:ROW], const_in[:, C_TBASE:C_TBASE + 2].unsqueeze(2))
            link(v.memset(first[0:1, 0:1], -1.0))
            bound = const_in[:, C_BOUND:C_BOUND + 2 * T * P]
            for c in range(2):
                last = v.tensor_scalar(sel[:, c], bound, first_next[:, c:c + 1], None, ALU.is_le)
            link(last)
            for c in range(2):
                last = v.scalar_tensor_tensor(sel[:, c], bound, first[:, c:c + 1], sel[:, c], ALU.is_gt, ALU.mult)
            last.then_inc(sel_ready, 1)
            v.tensor_copy(halo[:, :, 0:REACH], halo_i[:, :, 0:REACH])
            link(v.tensor_copy(halo[:, :, REACH + P:], halo_i[:, :, REACH + P:]))
            def equal(d):
                return v.tensor_tensor(same[d % 3][:, :, 0:P + d], halo[:, :, REACH - d:REACH + P],
                                       halo[:, :, REACH:REACH + P + d], ALU.is_equal).then_inc(count_chain, 1)

            equal(1)
            for d in range(1, REACH + 1):
                if d < REACH:
                    wait(dve, count_chain, 3 * d - 3)
                    equal(d + 1)
                for side, at in enumerate((d, 0)):
                    dve.wait_ge(count_chain, max(1, 3 * d - 3 + side))
                    v.tensor_tensor(count_side[side][:], count_side[side][:], same[d % 3][:, :, at:at + P],
                                    ALU.add).then_inc(count_chain, 1)
            dve.wait_ge(count_chain, 3 * REACH)
            link(v.tensor_tensor(count[:], count_side[0][:], count_side[1][:], ALU.add))
            link(v.tensor_scalar(recip[:], count[:], COUNT_EPS, None, ALU.add))
            link(v.reciprocal(recip[:], recip[:]))
            link(v.scalar_tensor_tensor(recip[:], count[:], 0.0, recip[:], ALU.is_gt, ALU.mult))
            v.tensor_tensor(mean_weight[:], weight_f[:], recip[:], ALU.mult).then_inc(table_in, 1)

            def windows():
                dve.wait_ge(table_T, 4)
                v.tensor_copy(dst_col[:], ps_u[:, 0:ET])
                link(v.tensor_copy(weight_col[:], ps_u[:, 256:256 + ET]))

                v.tensor_tensor(odd[:, 0], here, halo[:, :, REACH + 1:REACH + 1 + P], ALU.is_gt)
                link(v.tensor_tensor(odd[:, 1], here, halo[:, :, 2 * REACH:2 * REACH + P], ALU.is_equal))
                v.memset(odd[:, 2], 0.0)
                link(v.scalar_tensor_tensor(odd[:, 1], here, FAR, odd[:, 1], ALU.is_lt, ALU.mult))
                dve.wait_ge(sel_done, 1)
                for n in range(2 * T):
                    last = v.tensor_scalar(fine_out[:, n], sel_out(n)[:, 0:P],
                                           const_in[:, C_BOUNDC + n:C_BOUNDC + n + 1], None, ALU.is_lt, ALU.add,
                                           accum_out=fine[:, n:n + 1])
                link(last)
                for n in range(2 * T):
                    last = v.tensor_tensor(starts[:, n:n + 1], sel_out(n)[:, P:ROW], fine[:, n:n + 1], ALU.add)
                link(last)
                steps = const_in[:, C_WIN:C_WIN + T]
                v.tensor_tensor(ends[:], starts[:, T:2 * T], steps, ALU.subtract)
                link(v.tensor_tensor(starts[:, 0:T], starts[:, 0:T], steps, ALU.subtract))
                link(v.tensor_reduce(block_start[:], starts[:, 0:T], AX.X, ALU.min))
                link(v.tensor_scalar(ends[:], ends[:], float(P), block_start[:], ALU.subtract, ALU.is_gt))
                v.tensor_copy(odd[0:NB, 2, 0, 0:T], ends[0:NB])
                link(v.tensor_tensor(odd[0:NB, 2, 1, 0:1], block_start[0:NB], const_in[0:NB, C_LIMIT:C_LIMIT + 1],
                                     ALU.is_gt))
                v.tensor_reduce(odd_sum[:], odd[:].rearrange("p a b c -> p (a b c)"), AX.X, ALU.add).then_inc(
                    odd_ready, 1)
                v.tensor_scalar(block_start[:], block_start[:], float(EDGE0), None, ALU.add).then_inc(
                    block_starts_ready, 1)

            def general_and_starts():
                dve.wait_ge(odd_done, 1)
                link(v.tensor_scalar(general[:], ps_u[:, 1023:1024], 1.0, None, ALU.min))
                v.tensor_copy(general_i[:], general[:])
                dve.wait_ge(starts_T, 1)
                v.tensor_copy(start_row[:], ps_t[0:1, 0:P]).then_inc(starts_ready, 1)

            def by_row(column):
                return column.unsqueeze(2).to_broadcast([P, T, P])

            def z_norm(g, gh, gs):
                dve.wait_ge(z_rstd_ready, g + 1)
                wait(dve, e3_done, g)
                v.tensor_tensor(tiles(zn[:]), tiles(ps_z[:]), by_row(z_rstd[:]), ALU.mult).then_inc(zn_ready, 1)

            def rows(g, gh, gs):
                dve.wait_ge(e4_done, g + 1)
                wait(dve, rows_stored[gs], 16 * gh)
                r = msg_rows[gs][:].rearrange("p (j h) -> p j h", h=ROW)
                v.tensor_tensor(r[:, :, 0:P], tiles(ps_z[:]), by_row(weight_col[:, bass.ds(g * T, T)]), ALU.mult)
                v.tensor_copy(r[:, :, P:ROW], dst_col[:, bass.ds(g * T, T)].unsqueeze(2)).then_inc(rows_ready, 1)

            def dst_places(q, b, kh, ks):
                dve.wait_ge(win_loaded[2 * ks + b], 16 * 2 * (kh + 1))
                w = window[2 * ks + b][:].rearrange("p (j h) -> p j h", h=ROW)
                v.tensor_tensor(dst_place[b][:].unsqueeze(2), w[:, :, P:ROW],
                                tile_base[:, bass.ds(q * T, T)].unsqueeze(2), ALU.subtract).then_inc(place_chain, 1)

            def one_hots(q, b, kh, ks):
                dve.wait_ge(place_chain, q + 1)
                wait(dve, n2_done, 2 * q - 2)
                v.tensor_tensor(tiles(onehot[b][:]), iota_row.unsqueeze(1).to_broadcast([P, T, P]),
                                by_row(dst_place[b][:]), ALU.is_equal).then_inc(hot_ready, 1)

            def residual(q, b, kh, ks):
                gates = gate_small[b]
                dve.wait_ge(gate_chain, 2 * q + 2)
                v.scalar_tensor_tensor(gates[:, 2], gates[:, 1], 2.0, gates[:, 1], ALU.add, ALU.mult).then_inc(
                    y_chain, 1)
                dve.wait_ge(n4_done, q + 1)
                for j in range(T):
                    cols = slice(j * P, (j + 1) * P)
                    last = v.scalar_tensor_tensor(y[b][:, cols], ps_h[:, cols], gates[:, 1, j:j + 1],
                                                  x_rows[2 * ks + b][:, cols], ALU.mult, ALU.add)
                last.then_inc(y_ready, 1)

            def y_halves(q, b, kh, ks):
                dve.wait_ge(y_ready, q + 1)
                for j in range(T):
                    last = v.bn_stats(y_stats[b][:, j], y[b][:, j * P:(j + 1) * P])
                last.then_inc(y_chain, 1)

            def small_sums(y_block, gate_block):
                if gate_block is not None:
                    n, c = gate_block[:2]
                    dve.wait_ge(gate_exp_ready, n + 1)
                    v.tensor_scalar(gate_small[c][:, 0], gate_exp[c][:], 2.0, 1.0, ALU.mult, ALU.add).then_inc(
                        gate_chain, 1)
                if y_block is not None:
                    q, b = y_block[:2]
                    stats, small = y_stats[b], y_small[b]
                    dve.wait_ge(y_chain, 4 * q + 2)
                    v.tensor_tensor(small[:, 0], stats[:, :, 1], stats[:, :, 4], ALU.subtract)
                    v.scalar_tensor_tensor(small[:, 1], gate_small[b][:, 2], P * LN_EPS / 4, stats[:, :, 2],
                                           ALU.mult, ALU.add).then_inc(y_chain, 1)
                if gate_block is not None:
                    dve.wait_ge(gate_chain, 2 * n + 1)
                    v.reciprocal(gate_small[c][:, 1], gate_small[c][:, 0]).then_inc(gate_chain, 1)
                if y_block is not None:
                    dve.wait_ge(y_chain, 4 * q + 3)
                    v.scalar_tensor_tensor(small[:, 2], small[:, 0], P / 4.0, small[:, 0], ALU.mult, ALU.mult)
                    v.tensor_tensor(small[:, 3], small[:, 1], stats[:, :, 5], ALU.add).then_inc(y_chain, 1)
                    v.scalar_tensor_tensor(small[:, 5], small[:, 0], -0.5, stats[:, :, 1],
                                           ALU.mult, ALU.add).then_inc(y_mean_ready, 1)
                    dve.wait_ge(y_chain, 4 * q + 4)
                    v.tensor_tensor(small[:, 4], small[:, 2], small[:, 3], ALU.add).then_inc(y_var_ready, 1)

            def result(q, b, kh, ks):
                dve.wait_ge(y_rstd_ready, q + 1)
                dve.wait_ge(y_mean_ready, q + 1)
                wait(dve, out_stored[b], 16 * (2 * kh + ks))
                for j in range(T):
                    cols = slice(j * P, (j + 1) * P)
                    last = v.tensor_scalar(out_rows[b][:, cols], y[b][:, cols], y_small[b][:, 5, j:j + 1],
                                           y_rstd[b][:, j:j + 1], ALU.subtract, ALU.mult)
                last.then_inc(out_ready, 1)

            def step(g, gh, gs, k, kh, ks):
                this, former = group(g, gh, gs, 0), group(g, gh, gs, 1)
                for b in range(2):
                    at = [behind(k, kh, ks, b, n) if k is not None else None for n in range(4)]
                    if b == 0:
                        on(dst_places, at[0])
                    on(one_hots, at[0])
                    on(result, at[3])
                    on(residual, at[2])
                    on(y_halves, at[2])
                    on(*((rows, former) if b == 0 else (z_norm, this)))
                    if b == 0 and k is not None:
                        on(dst_places, behind(k, kh, ks, 1, 0))
                    small_sums(at[2], at[1])

            def sum_by_node():
                v.memset(xT[0][:], 0.0).then_inc(zeros_ready, 1)
                for j in range(T):
                    v.tensor_scalar(block_nodes[:, j * P:(j + 1) * P], iota_row, float(j * P), None, ALU.add)
                    last = v.tensor_scalar(node_col[:, j:j + 1], const_in[:, C_TBASE:C_TBASE + 1], 1.0 / P,
                                           float(j * P), ALU.mult, ALU.add)
                last.then_inc(sum_chain, 1)
                with dve.Fori(0, NB) as q:
                    with dve.Fori(0, EG) as g:
                        dve.wait_ge(sum_chain, 5 * q + 1)
                        dve.wait_ge(group_loaded, q * (16 * EG) + g * 16 + 16)
                        for i in range(T):
                            last = v.tensor_scalar(sum_hot[i][:], block_nodes[:],
                                                   window[0][:, i * ROW + P:(i + 1) * ROW], None, ALU.is_equal)
                        last.then_inc(group_hot, 1)
                    dve.wait_ge(block_summed, q + 1)
                    dve.wait_ge(sums_stored, q * 16 + 16)
                    v.tensor_scalar(node_recip[:, 0], ps_x[:, 0:T], COUNT_EPS, None, ALU.add).then_inc(sum_chain, 1)
                    dve.wait_ge(sum_chain, 5 * q + 2)
                    v.reciprocal(node_recip[:, 1], node_recip[:, 0]).then_inc(sum_chain, 1)
                    dve.wait_ge(sum_chain, 5 * q + 3)
                    v.scalar_tensor_tensor(node_recip[:, 2], ps_x[:, 0:T], 0.0, node_recip[:, 1],
                                           ALU.is_gt, ALU.mult).then_inc(sum_chain, 1)
                    dve.wait_ge(sum_chain, 5 * q + 4)
                    r = msg_rows[0][:].rearrange("p (j h) -> p j h", h=ROW)
                    v.tensor_tensor(r[:, :, 0:P], tiles(ps_t[:]), by_row(node_recip[:, 2]), ALU.mult).then_inc(
                        sums_read, 1)
                    v.tensor_copy(r[:, :, P:ROW], node_col[:].unsqueeze(2)).then_inc(sums_ready, 1)
                    v.tensor_scalar(block_nodes[:], block_nodes[:], float(BN), None, ALU.add).then_inc(sum_chain, 1)
                    dve.wait_ge(sums_ready, q + 1)
                    v.tensor_scalar(node_col[:], node_col[:], float(BN), None, ALU.add).then_inc(sum_chain, 1)

            head(dve, step, (windows, general_and_starts))
            with is_general(dve):
                restart(dve, 1)
                dve.wait_ge(weight_T, 1)
                link(v.tensor_copy(weight_col[:], ps_u[:, 0:ET]))
                all_edges(dve, step)
                sum_by_node()
                restart(dve, 2)
                head(dve, step)
            rest(dve, step)


def constants(n_nodes):
    blocks = -(-n_nodes // (T * P))
    wt = blocks * T
    at = const_columns(wt)
    c = np.zeros((P, at[-1]), np.float32)
    rows = np.arange(P, dtype=np.float32)
    firsts = np.concatenate([min(q * T * P, n_nodes - T * P) + P * np.arange(T) for q in range(blocks)])
    by_tile = np.zeros((2, T, P))
    by_tile[0, :, :blocks] = firsts.reshape(blocks, T).T
    by_tile[1, :, :blocks] = by_tile[0, :, :blocks] + P
    by_tile = by_tile.reshape(2 * T, P)
    pair = np.arange(P) // 2
    limit = np.where(pair + 2 >= blocks // 2, float(n_nodes), (pair + 2) * T * P - SPAN)
    c[:, at[0]:at[1]] = np.eye(P)
    c[:, at[1]:at[2]] = rows[None, :]
    c[:, at[2]:at[3]] = by_tile.reshape(1, -1)
    c[:, at[3]:at[4]] = by_tile.T
    c[:, at[4]] = rows * P
    c[:, at[4] + 1] = (rows + P) * P
    c[:, at[5]:at[6]] = firsts[None, :]
    c[:, at[6]:at[7]] = np.eye(P)[:, :3]
    c[:, at[7]] = limit
    c[:, at[8]:at[9]] = HALF * np.arange(T)[None, :]
    return c


_INS = ["x", "src", "dst", "edge_weight", "L0_gnn_msg_w", "L0_gnn_msg_b", "L0_gnn_msg_g", "L0_gnn_msg_beta",
        "L0_gnn_upd_w", "L0_gnn_upd_b", "L0_gnn_upd_g", "L0_gnn_upd_beta", "L0_gnn_gate_w", "L0_gnn_gate_b"]


def kernel(**inputs):
    import concourse.bacc as _bacc
    from concourse.bass_utils import run_bass_kernel_spmd as _run

    nc = _bacc.Bacc("TRN2", target_bir_lowering=False, num_devices=1)
    arrays, args = {}, []
    given = [(name, np.ascontiguousarray(inputs[name])) for name in _INS]
    given.append(("constants", constants(inputs["x"].shape[0])))
    for name, a in given:
        arrays[f"in_{name}"] = a
        args.append(nc.dram_tensor(f"in_{name}", a.shape, mybir.dt.from_np(a.dtype), kind="ExternalInput").ap())
    args.append(nc.dram_tensor("out_0", inputs["x"].shape, F32, kind="ExternalOutput").ap())
    gnn_kernel(nc, *args)
    r = _run(nc, [arrays], core_ids=[0])
    return r.results[0]["out_0"]
```
